# Optimizing a Trainium2 kernel written in Bass

```python
import numpy as np
import jax
import jax.numpy as jnp

def _softmax(x, axis=-1):
    return jax.nn.softmax(x, axis=axis)

def _gelu(x):
    return jax.nn.gelu(x, approximate=True)

def _silu(x):
    return jax.nn.silu(x)

def _sigmoid(x):
    return jax.nn.sigmoid(x)

def _layernorm(x, axis=-1, eps=1e-05):
    m = jnp.mean(x, axis=axis, keepdims=True)
    v = jnp.var(x, axis=axis, keepdims=True)
    return (x - m) / jnp.sqrt(v + eps)

def _scatter_add(tgt, idx, src, axis=0):
    return tgt.at[idx].add(src)

def _segment_sum(src, seg, n):
    return jax.ops.segment_sum(src, seg, n)
kernel_name = 'mk_gnn_resnorm_d4_gnn_r16_df1ee5'

def setup_inputs(seed: int=0):
    np.random.seed(seed)
    _w = jnp.asarray

    def _rec_inputs():
        import jax
        import jax.numpy as jnp
        _gk = jax.random.key(seed)
        x = -0.0003713 + 1 * jax.random.normal(jax.random.fold_in(_gk, 1), (6250, 128), jnp.float32)
        _s = jax.random.randint(jax.random.fold_in(_gk, 2), (50000,), 0, 6250, jnp.int32)
        _d = jax.random.randint(jax.random.fold_in(_gk, 3), (50000,), 0, 6250, jnp.int32)
        _loop = jnp.arange(6250, dtype=jnp.int32)
        src = jnp.concatenate([_s, _d, _loop])
        dst = jnp.concatenate([_d, _s, _loop])
        _o = jnp.argsort(dst, stable=True)
        src = src[_o]
        dst = dst[_o]
        edge_attr_128 = 5.93493e-05 + 1.00006 * jax.random.normal(jax.random.fold_in(_gk, 13), (106250, 128), jnp.float32)
        edge_attr_3 = 0.000669165 + 0.999965 * jax.random.normal(jax.random.fold_in(_gk, 14), (106250, 3), jnp.float32)
        return (x, src, dst, edge_attr_128, edge_attr_3)
    x, src, dst, edge_attr_128, edge_attr_3 = _rec_inputs()

    def _L0_gnn_setup():
        import jax, jax.numpy as jnp
        import numpy as np
        N = 6250
        E = 100000
        DIN = 128
        DOUT = 128
        NEG_SLOPE = 0.2
        key = jax.random.key(seed)
        k1, k2, k3, k4, k5, k6 = jax.random.split(key, 6)
        h = jax.random.normal(k1, (N, DIN), dtype=jnp.float32)
        src = jax.random.randint(k2, (E,), 0, N, dtype=jnp.int32)
        dst = jax.random.randint(k3, (E,), 0, N, dtype=jnp.int32)
        W = jax.random.normal(k4, (DIN, DOUT), dtype=jnp.float32) / np.sqrt(DIN).astype(np.float32)
        attn_l = jax.random.normal(k5, (DOUT,), dtype=jnp.float32) * 0.1
        attn_r = jax.random.normal(k6, (DOUT,), dtype=jnp.float32) * 0.1
        return {'h': h, 'src': src, 'dst': dst, 'W': W, 'attn_l': attn_l, 'attn_r': attn_r}
    _L0_gnn_all = _L0_gnn_setup()
    _L0_gnn_in = {k: v for k, v in _L0_gnn_all.items() if k in ('W', 'attn_l', 'attn_r')}
    del _L0_gnn_all

    def _L1_gnn_setup():
        import jax, jax.numpy as jnp
        import numpy as np
        N_NODES = 6250
        N_EDGES = 37500
        HIDDEN = 128
        key = jax.random.key(seed)
        ks = jax.random.split(key, 12)
        s = 0.05
        x = jax.random.normal(ks[0], (N_NODES, HIDDEN), dtype=jnp.float32)
        edge_index = jax.random.randint(ks[1], (2, N_EDGES), 0, N_NODES, dtype=jnp.int64)
        edge_features = jax.random.normal(ks[2], (N_EDGES, HIDDEN), dtype=jnp.float32)
        global_feat = jax.random.normal(ks[3], (1, HIDDEN), dtype=jnp.float32)
        W_c = jax.random.normal(ks[4], (3 * HIDDEN, HIDDEN), dtype=jnp.float32) * s
        b_c = jnp.zeros((HIDDEN,), dtype=jnp.float32)
        W1 = jax.random.normal(ks[5], (HIDDEN, HIDDEN), dtype=jnp.float32) * s
        b1 = jnp.zeros((HIDDEN,), dtype=jnp.float32)
        W2 = jax.random.normal(ks[6], (HIDDEN, HIDDEN), dtype=jnp.float32) * s
        b2 = jnp.zeros((HIDDEN,), dtype=jnp.float32)
        W3 = jax.random.normal(ks[7], (HIDDEN, HIDDEN), dtype=jnp.float32) * s
        b3 = jnp.zeros((HIDDEN,), dtype=jnp.float32)
        return {'x': x, 'edge_index': edge_index, 'edge_features': edge_features, 'global_feat': global_feat, 'W_c': W_c, 'b_c': b_c, 'W1': W1, 'b1': b1, 'W2': W2, 'b2': b2, 'W3': W3, 'b3': b3}
    _L1_gnn_all = _L1_gnn_setup()
    _L1_gnn_in = {k: v for k, v in _L1_gnn_all.items() if k in ('global_feat', 'W_c', 'b_c', 'W1', 'b1', 'W2', 'b2', 'W3', 'b3')}
    del _L1_gnn_all

    def _L2_gnn_setup():
        import jax, jax.numpy as jnp
        import numpy as np
        N, E, IN, H, ED = (3125, 50000, 128, 128, 3)
        EPS = 1e-05

        def _gat_conv(x, src, dst, ea, W, a_src, a_dst, We, a_edge, bias):
            n = x.shape[0]
            loops = jnp.arange(n, dtype=src.dtype)
            s = jnp.concatenate([src, loops])
            d = jnp.concatenate([dst, loops])
            ea_full = jnp.concatenate([ea, jnp.broadcast_to(ea.mean(0), (n, ea.shape[1]))], 0)
            h = x @ W
            al_s = h @ a_src
            al_d = h @ a_dst
            al_e = ea_full @ We @ a_edge
            alpha = jax.nn.leaky_relu(al_s[s] + al_d[d] + al_e, 0.2)
            amax = jax.ops.segment_max(alpha, d, num_segments=n)
            ex = jnp.exp(alpha - amax[d])
            denom = jax.ops.segment_sum(ex, d, num_segments=n)
            coef = ex / (denom[d] + 1e-16)
            out = jax.ops.segment_sum(h[s] * coef[:, None], d, num_segments=n)
            return out + bias

        def _bn(x, gamma, beta):
            mu = x.mean(0)
            var = ((x - mu) ** 2).mean(0)
            return (x - mu) * jax.lax.rsqrt(var + EPS) * gamma + beta
        key = jax.random.key(seed)
        ks = jax.random.split(key, 40)
        inp = {'x': jax.random.normal(ks[0], (N, IN), jnp.float32), 'edge_index': jax.random.randint(ks[1], (2, E), 0, N, dtype=jnp.int32), 'batch': jnp.zeros((N,), jnp.int32), 'edge_attr': jax.random.normal(ks[2], (E, ED), jnp.float32)}
        i = 3
        for l, cin in ((1, IN), (2, H), (3, H)):
            s = 1.0 / np.sqrt(cin)
            inp[f'W{l}'] = jax.random.normal(ks[i], (cin, H), jnp.float32) * s
            i += 1
            inp[f'as{l}'] = jax.random.normal(ks[i], (H,), jnp.float32) * 0.1
            i += 1
            inp[f'ad{l}'] = jax.random.normal(ks[i], (H,), jnp.float32) * 0.1
            i += 1
            inp[f'We{l}'] = jax.random.normal(ks[i], (ED, H), jnp.float32) * 0.5
            i += 1
            inp[f'ae{l}'] = jax.random.normal(ks[i], (H,), jnp.float32) * 0.1
            i += 1
            inp[f'b{l}'] = jnp.zeros((H,), jnp.float32)
            inp[f'g{l}'] = jnp.ones((H,), jnp.float32)
            inp[f'be{l}'] = jnp.zeros((H,), jnp.float32)
        return inp
    _L2_gnn_all = _L2_gnn_setup()
    _L2_gnn_in = {k: v for k, v in _L2_gnn_all.items() if k in ('W1', 'as1', 'ad1', 'We1', 'ae1', 'b1', 'g1', 'be1', 'W2', 'as2', 'ad2', 'We2', 'ae2', 'b2', 'g2', 'be2', 'W3', 'as3', 'ad3', 'We3', 'ae3', 'b3', 'g3', 'be3')}
    del _L2_gnn_all

    def _L3_gnn_setup():
        import jax, jax.numpy as jnp
        import numpy as np
        L = 5
        D = 128
        BN_EPS = 1e-05

        def _bn(x, g, b):
            m = jnp.mean(x, axis=0)
            v = jnp.var(x, axis=0)
            return g * (x - m) * jax.lax.rsqrt(v + BN_EPS) + b
        key = jax.random.key(seed)
        ks = jax.random.split(key, 12)
        N, E = (3125, 50000)
        h = jax.random.normal(ks[0], (N, D), dtype=jnp.float32)
        src = jax.random.randint(ks[1], (E,), 0, N)
        dst = jax.random.randint(ks[2], (E,), 0, N)
        s = 1.0 / np.sqrt(D)
        W1 = jax.random.uniform(ks[3], (L, D, D), jnp.float32, -s, s)
        b1 = jax.random.uniform(ks[4], (L, D), jnp.float32, -s, s)
        W2 = jax.random.uniform(ks[5], (L, D, D), jnp.float32, -s, s)
        b2 = jax.random.uniform(ks[6], (L, D), jnp.float32, -s, s)
        bn1_g = jax.random.uniform(ks[7], (L, D), jnp.float32, 0.5, 1.5)
        bn1_b = jax.random.normal(ks[8], (L, D), jnp.float32) * 0.1
        bn2_g = jax.random.uniform(ks[9], (L, D), jnp.float32, 0.5, 1.5)
        bn2_b = jax.random.normal(ks[10], (L, D), jnp.float32) * 0.1
        bn3_g = jax.random.uniform(ks[11], (L, D), jnp.float32, 0.5, 1.5)
        bn3_b = jnp.zeros((L, D), jnp.float32)
        return dict(h=h, src=src, dst=dst, W1=W1, b1=b1, W2=W2, b2=b2, bn1_g=bn1_g, bn1_b=bn1_b, bn2_g=bn2_g, bn2_b=bn2_b, bn3_g=bn3_g, bn3_b=bn3_b)
    _L3_gnn_all = _L3_gnn_setup()
    _L3_gnn_in = {k: v for k, v in _L3_gnn_all.items() if k in ('W1', 'b1', 'W2', 'b2', 'bn1_g', 'bn1_b', 'bn2_g', 'bn2_b', 'bn3_g', 'bn3_b')}
    del _L3_gnn_all
    return {'x': x, 'src': src, 'dst': dst, 'edge_attr_128': edge_attr_128, 'edge_attr_3': edge_attr_3, 'L0_gnn_W': _L0_gnn_in['W'], 'L0_gnn_attn_l': _L0_gnn_in['attn_l'], 'L0_gnn_attn_r': _L0_gnn_in['attn_r'], 'L1_gnn_global_feat': _L1_gnn_in['global_feat'], 'L1_gnn_W_c': _L1_gnn_in['W_c'], 'L1_gnn_b_c': _L1_gnn_in['b_c'], 'L1_gnn_W1': _L1_gnn_in['W1'], 'L1_gnn_b1': _L1_gnn_in['b1'], 'L1_gnn_W2': _L1_gnn_in['W2'], 'L1_gnn_b2': _L1_gnn_in['b2'], 'L1_gnn_W3': _L1_gnn_in['W3'], 'L1_gnn_b3': _L1_gnn_in['b3'], 'L2_gnn_W1': _L2_gnn_in['W1'], 'L2_gnn_as1': _L2_gnn_in['as1'], 'L2_gnn_ad1': _L2_gnn_in['ad1'], 'L2_gnn_We1': _L2_gnn_in['We1'], 'L2_gnn_ae1': _L2_gnn_in['ae1'], 'L2_gnn_b1': _L2_gnn_in['b1'], 'L2_gnn_g1': _L2_gnn_in['g1'], 'L2_gnn_be1': _L2_gnn_in['be1'], 'L2_gnn_W2': _L2_gnn_in['W2'], 'L2_gnn_as2': _L2_gnn_in['as2'], 'L2_gnn_ad2': _L2_gnn_in['ad2'], 'L2_gnn_We2': _L2_gnn_in['We2'], 'L2_gnn_ae2': _L2_gnn_in['ae2'], 'L2_gnn_b2': _L2_gnn_in['b2'], 'L2_gnn_g2': _L2_gnn_in['g2'], 'L2_gnn_be2': _L2_gnn_in['be2'], 'L2_gnn_W3': _L2_gnn_in['W3'], 'L2_gnn_as3': _L2_gnn_in['as3'], 'L2_gnn_ad3': _L2_gnn_in['ad3'], 'L2_gnn_We3': _L2_gnn_in['We3'], 'L2_gnn_ae3': _L2_gnn_in['ae3'], 'L2_gnn_b3': _L2_gnn_in['b3'], 'L2_gnn_g3': _L2_gnn_in['g3'], 'L2_gnn_be3': _L2_gnn_in['be3'], 'L3_gnn_W1': _L3_gnn_in['W1'], 'L3_gnn_b1': _L3_gnn_in['b1'], 'L3_gnn_W2': _L3_gnn_in['W2'], 'L3_gnn_b2': _L3_gnn_in['b2'], 'L3_gnn_bn1_g': _L3_gnn_in['bn1_g'], 'L3_gnn_bn1_b': _L3_gnn_in['bn1_b'], 'L3_gnn_bn2_g': _L3_gnn_in['bn2_g'], 'L3_gnn_bn2_b': _L3_gnn_in['bn2_b'], 'L3_gnn_bn3_g': _L3_gnn_in['bn3_g'], 'L3_gnn_bn3_b': _L3_gnn_in['bn3_b']}

def reference(x, src, dst, edge_attr_128, edge_attr_3, L0_gnn_W, L0_gnn_attn_l, L0_gnn_attn_r, L1_gnn_global_feat, L1_gnn_W_c, L1_gnn_b_c, L1_gnn_W1, L1_gnn_b1, L1_gnn_W2, L1_gnn_b2, L1_gnn_W3, L1_gnn_b3, L2_gnn_W1, L2_gnn_as1, L2_gnn_ad1, L2_gnn_We1, L2_gnn_ae1, L2_gnn_b1, L2_gnn_g1, L2_gnn_be1, L2_gnn_W2, L2_gnn_as2, L2_gnn_ad2, L2_gnn_We2, L2_gnn_ae2, L2_gnn_b2, L2_gnn_g2, L2_gnn_be2, L2_gnn_W3, L2_gnn_as3, L2_gnn_ad3, L2_gnn_We3, L2_gnn_ae3, L2_gnn_b3, L2_gnn_g3, L2_gnn_be3, L3_gnn_W1, L3_gnn_b1, L3_gnn_W2, L3_gnn_b2, L3_gnn_bn1_g, L3_gnn_bn1_b, L3_gnn_bn2_g, L3_gnn_bn2_b, L3_gnn_bn3_g, L3_gnn_bn3_b):
    import jax
    import jax.numpy as jnp

    def _L0_gnn_ref(h, src, dst, W, attn_l, attn_r):
        import jax, jax.numpy as jnp
        import numpy as np
        N = 6250
        E = 100000
        DIN = 128
        DOUT = 128
        NEG_SLOPE = 0.2
        feat = h @ W
        el = feat @ attn_l
        er = feat @ attn_r
        e = jax.nn.leaky_relu(el[src] + er[dst], NEG_SLOPE)
        m = jax.ops.segment_max(e, dst, num_segments=N)
        m = jnp.where(jnp.isfinite(m), m, 0.0)
        ex = jnp.exp(e - m[dst])
        denom = jax.ops.segment_sum(ex, dst, num_segments=N)
        alpha = ex / jnp.maximum(denom[dst], jnp.float32(1e-09))
        out = jax.ops.segment_sum(alpha[:, None] * feat[src], dst, num_segments=N)
        return out

    def _L1_gnn_ref(x, edge_index, edge_features, global_feat, W_c, b_c, W1, b1, W2, b2, W3, b3):
        import jax, jax.numpy as jnp
        import numpy as np
        N_NODES = 6250
        N_EDGES = 37500
        HIDDEN = 128
        n = x.shape[0]
        row = edge_index[0]
        edge_aggr = jnp.zeros((n, HIDDEN), dtype=x.dtype).at[row].add(edge_features)
        reps = n // global_feat.shape[0]
        global_expand = jnp.repeat(global_feat, reps, axis=0)
        combined = jnp.concatenate([x, edge_aggr, global_expand], axis=-1) @ W_c + b_c
        h = jax.nn.softplus(combined @ W1 + b1)
        h = jax.nn.softplus(h @ W2 + b2)
        return h @ W3 + b3

    def _L2_gnn_ref(x, edge_index, batch, edge_attr, W1, as1, ad1, We1, ae1, b1, g1, be1, W2, as2, ad2, We2, ae2, b2, g2, be2, W3, as3, ad3, We3, ae3, b3, g3, be3):
        import jax, jax.numpy as jnp
        import numpy as np
        N, E, IN, H, ED = (3125, 50000, 128, 128, 3)
        EPS = 1e-05

        def _gat_conv(x, src, dst, ea, W, a_src, a_dst, We, a_edge, bias):
            n = x.shape[0]
            loops = jnp.arange(n, dtype=src.dtype)
            s = jnp.concatenate([src, loops])
            d = jnp.concatenate([dst, loops])
            ea_full = jnp.concatenate([ea, jnp.broadcast_to(ea.mean(0), (n, ea.shape[1]))], 0)
            h = x @ W
            al_s = h @ a_src
            al_d = h @ a_dst
            al_e = ea_full @ We @ a_edge
            alpha = jax.nn.leaky_relu(al_s[s] + al_d[d] + al_e, 0.2)
            amax = jax.ops.segment_max(alpha, d, num_segments=n)
            ex = jnp.exp(alpha - amax[d])
            denom = jax.ops.segment_sum(ex, d, num_segments=n)
            coef = ex / (denom[d] + 1e-16)
            out = jax.ops.segment_sum(h[s] * coef[:, None], d, num_segments=n)
            return out + bias

        def _bn(x, gamma, beta):
            mu = x.mean(0)
            var = ((x - mu) ** 2).mean(0)
            return (x - mu) * jax.lax.rsqrt(var + EPS) * gamma + beta
        src, dst = (edge_index[0], edge_index[1])
        h = _gat_conv(x, src, dst, edge_attr, W1, as1, ad1, We1, ae1, b1)
        h = _bn(jax.nn.leaky_relu(h, 0.01), g1, be1)
        h = _gat_conv(h, src, dst, edge_attr, W2, as2, ad2, We2, ae2, b2)
        h = _bn(jax.nn.leaky_relu(h, 0.01), g2, be2)
        h = _gat_conv(h, src, dst, edge_attr, W3, as3, ad3, We3, ae3, b3)
        h = _bn(jax.nn.leaky_relu(h, 0.01), g3, be3)
        return h

    def _L3_gnn_ref(h, src, dst, W1, b1, W2, b2, bn1_g, bn1_b, bn2_g, bn2_b, bn3_g, bn3_b):
        import jax, jax.numpy as jnp
        import numpy as np
        L = 5
        D = 128
        BN_EPS = 1e-05

        def _bn(x, g, b):
            m = jnp.mean(x, axis=0)
            v = jnp.var(x, axis=0)
            return g * (x - m) * jax.lax.rsqrt(v + BN_EPS) + b
        N = h.shape[0]
        for l in range(L):
            agg = jax.ops.segment_sum(h[src], dst, num_segments=N)
            rst = h + agg
            x = rst @ W1[l] + b1[l]
            x = jax.nn.relu(_bn(x, bn1_g[l], bn1_b[l]))
            x = x @ W2[l] + b2[l]
            x = jax.nn.relu(_bn(x, bn2_g[l], bn2_b[l]))
            h = jax.nn.relu(_bn(x, bn3_g[l], bn3_b[l]))
        return h
    edge_index = jnp.stack([src, dst])
    batch0 = jnp.zeros((6250,), jnp.int32)
    x = _layernorm(x + _L0_gnn_ref(x, src, dst, L0_gnn_W, L0_gnn_attn_l, L0_gnn_attn_r), axis=-1)
    x = _layernorm(x + _L1_gnn_ref(x, edge_index, edge_attr_128, L1_gnn_global_feat, L1_gnn_W_c, L1_gnn_b_c, L1_gnn_W1, L1_gnn_b1, L1_gnn_W2, L1_gnn_b2, L1_gnn_W3, L1_gnn_b3), axis=-1)
    x = _layernorm(x + _L2_gnn_ref(x, edge_index, batch0, edge_attr_3, L2_gnn_W1, L2_gnn_as1, L2_gnn_ad1, L2_gnn_We1, L2_gnn_ae1, L2_gnn_b1, L2_gnn_g1, L2_gnn_be1, L2_gnn_W2, L2_gnn_as2, L2_gnn_ad2, L2_gnn_We2, L2_gnn_ae2, L2_gnn_b2, L2_gnn_g2, L2_gnn_be2, L2_gnn_W3, L2_gnn_as3, L2_gnn_ad3, L2_gnn_We3, L2_gnn_ae3, L2_gnn_b3, L2_gnn_g3, L2_gnn_be3), axis=-1)
    x = _layernorm(x + _L3_gnn_ref(x, src, dst, L3_gnn_W1, L3_gnn_b1, L3_gnn_W2, L3_gnn_b2, L3_gnn_bn1_g, L3_gnn_bn1_b, L3_gnn_bn2_g, L3_gnn_bn2_b, L3_gnn_bn3_g, L3_gnn_bn3_b), axis=-1)
    return x

_drawn_inputs = setup_inputs


def setup_inputs(seed=0):
    import zlib

    import numpy as np

    out = dict(_drawn_inputs(seed))
    spreads = {'L1_gnn_b_c': (0.0, 0.1),
     'L1_gnn_b1': (0.0, 0.1),
     'L1_gnn_b2': (0.0, 0.1),
     'L1_gnn_b3': (0.0, 0.1),
     'L2_gnn_b1': (0.0, 0.1),
     'L2_gnn_g1': (1.0, 0.2),
     'L2_gnn_be1': (0.0, 0.1),
     'L2_gnn_b2': (0.0, 0.1),
     'L2_gnn_g2': (1.0, 0.2),
     'L2_gnn_be2': (0.0, 0.1),
     'L2_gnn_b3': (0.0, 0.1),
     'L2_gnn_g3': (1.0, 0.2),
     'L2_gnn_be3': (0.0, 0.1),
     'L3_gnn_bn3_b': (0.0, 0.1)}
    factors = {}
    for name, (base, spread) in spreads.items():
        noise = np.random.default_rng([zlib.crc32(name.encode()), seed]).standard_normal(out[name].shape)
        drawn = base * np.exp(spread * noise) if base else spread * noise
        out[name] = jnp.asarray(drawn.astype(out[name].dtype))
    for name, factor in factors.items():
        out[name] = (out[name] * factor).astype(out[name].dtype)
    return out
```

```python
from contextlib import ExitStack

import concourse.bass as bass
from concourse import mybir

F32 = mybir.dt.float32
BF16 = mybir.dt.bfloat16
I32 = mybir.dt.int32
ALU = mybir.AluOpType
ACT = mybir.ActivationFunctionType
AX = mybir.AxisListType

P = 128
N = 6250
E = 106250
D = 128
NB = -(-N // P)
GB = 5
NBP = -(-NB // (2 * GB)) * 2 * GB
NP = NBP * P
T = -(-E // P)
TP = T + 1
U = 16
G = 4
NG = U // G
K = -(-(T + NB - 1) // U) * U
KJ = -(-K // P)
KP = KJ * P
ITER = K // U
C = D + 4
DEN, MAX, ER = D, D + 1, D + 2
R = D + 1
CH = 400
NCH = NP // CH
BIG = -1.0e30
EPS = 1e-5
GIN = 5
TABLES = 4
L1U = 8
L1I = -(-T // (2 * L1U))
PAD_DST = NBP * P
L2VECS = ("b", "g", "be")
GVECS = ("b1", "b2", "bn1_g", "bn1_b", "bn2_g", "bn2_b", "bn3_g", "bn3_b")


def build(nc, a, out):
    ctx = ExitStack()
    with ctx:
        pe, dve, act, pool, sp = nc.tensor, nc.vector, nc.scalar, nc.gpsimd, nc.sync

        def sb(name, cols, dt=F32, parts=P):
            return ctx.enter_context(nc.sbuf_tensor(name, [parts, cols], dt))

        def dram(name, shape, dt=F32):
            return nc.dram_tensor(name, shape, dt).ap()

        src_pad = dram("src_pad", (TP, P), I32)
        dst_pad = dram("dst_pad", (TP, P), I32)
        ea3_pad = dram("ea3_pad", (TP, P * 3))
        idx_steps = dram("idx_steps", (K // G, P, G), I32)
        dloc_rows = dram("dloc_rows", (KP, P), BF16)
        tail_rows = dram("tail_rows", (L1U * P, D))
        gat_rows = dram("gat_rows", (NP, R))
        gin_rows = dram("gin_rows", (NP, D))
        sums = [dram(f"edge_sums{t}", (NP, D)) for t in range(TABLES)]

        X = sb("x_nodes", NBP * D)
        S = sb("state", NBP * C)
        XTa = sb("xT_a", NP)
        XTb = sb("xT_b", NP)
        dloc_cols = sb("dloc_cols", KP)
        al_cols = sb("al_cols", 4 * KP)
        btab = sb("block_of_step", U + KP, I32, 1)
        ident = sb("ident", P)
        ones = sb("ones", P)
        lower = sb("lower", P)
        iota_p = sb("iota_p", 1)
        dump = sb("dump", 1)
        iota_row = sb("iota_row", P)
        Wst = sb("w_static", 8 * D)
        Wext = sb("w_ext", 4 * (D + 2))
        vec = sb("vectors", 128)
        aff = sb("affine", 2)
        stat = sb("stats", 6 * 16)
        small = sb("small", 64)
        aloop = sb("aloop", 3)
        rows5 = [sb(f"rows5_{h}", GB * D) for h in range(2)]
        gst = [sb(f"gat_stage{h}", GB * R) for h in range(2)]
        idx = [sb(f"idx{g}", G, I32) for g in range(NG)]
        grow = [sb(f"grow{g}", G * R) for g in range(NG)]
        dl = [sb(f"dl{g}", G * P, BF16) for g in range(NG)]
        mask = [sb(f"mask{g}", G * P, BF16) for g in range(NG)]
        s_col = [sb(f"s_col{g}", G) for g in range(NG)]
        sm = [sb(f"sm{i}", P + 2) for i in range(4)]
        um = [sb(f"um{i}", P + 2) for i in range(2)]
        neg = [sb(f"neg{i}", 1) for i in range(2)]
        pt = [sb(f"pt{i}", P + 2) for i in range(8)]
        colst = [sb(f"col_stage{h}", L1U) for h in range(2)]
        pw = [sb(f"pw{i}", P) for i in range(4)]
        PS = ctx.enter_context(nc.psum_tensor("ps", [P, 8 * 512], F32))

        def bank(i, cols=512, n=1):
            return PS[:, i * 512:i * 512 + cols] if n == 1 else PS[:, i * 512:(i + n) * 512]

        sems = {}
        for name in ("chain", "load", "load2", "store", "stage", "mm", "evac", "out",
                     "s_ready", "bcast", "old_max", "masked", "new_max", "weights", "transposed",
                     "pw_ready", "product", "summed", "leaky", "act_a", "act_b", "m_ready",
                     "rows0", "rows1", "rows2", "rows3", "idx0", "idx1", "idx2", "idx3",
                     "dl0", "dl1", "dl2", "dl3", "tab0", "tab1", "tab2", "tab3",
                     "eq", "first", "index", "open", "ld0", "ld1", "st0", "st1", "base", "memset"):
            sems[name] = ctx.enter_context(nc.semaphore(name))
        sem_list = list(sems.values())
        q = sems
        sem_range = range(min(s.num for s in sem_list), max(s.num for s in sem_list) + 1)
        assert len(sem_range) == len(sem_list)

        def end_phase(pool_dmas=()):
            for name, count in pool_dmas:
                pool.wait_ge(q[name], count)
            if pool_dmas:
                pool.dma_reset(sem_range)
            nc.all_engine_barrier(sems_to_clear=sem_range)

        def settled(eng):
            eng.sem_inc(q["open"], 1)

        class Serial:

            def __init__(self):
                self.counts = {"chain": 0, "load2": 0}
                self.last = None

            def wait(self, eng):
                if self.last:
                    eng.wait_ge(q[self.last], self.counts[self.last])

            def __call__(self, eng, ins, inc=1):
                name = "load2" if eng is pool and inc == 16 else "chain"
                self.wait(eng)
                ins().then_inc(q[name], inc)
                self.counts[name] += inc
                self.last = name

        def xb(t, c=D):
            return t[:, :].rearrange("p (b c) -> p b c", c=c)

        Xb, Sb = xb(X), xb(S, C)
        row = lambda v: v.rearrange("(a n) -> a n", a=1)
        col = lambda v: v.rearrange("(n a) -> n a", a=1)

        VB = {}

        def vcol(name):
            if name not in VB:
                VB[name] = len(VB)
            return vec[:, VB[name]:VB[name] + 1]

        s = Serial()
        s(pool, lambda: pool.memset(ones[:, :], 1.0))
        s(pool, lambda: pool.memset(ident[:, :], 0.0))
        s(pool, lambda: pool.affine_select(out=ident[:, :], in_=ident[:, :], compare_op=ALU.not_equal,
                                           fill=1.0, base=0, pattern=[[-1, P]], channel_multiplier=1))
        s(pool, lambda: pool.affine_select(out=lower[:, :], in_=ones[:, :], compare_op=ALU.is_gt,
                                           fill=0.0, base=0, pattern=[[-1, P]], channel_multiplier=1))
        s(pool, lambda: pool.iota(iota_p[:, :], pattern=[[0, 1]], base=0, channel_multiplier=1,
                                  allow_small_or_imprecise_dtypes=True))
        s(pool, lambda: pool.iota(dump[:, :], pattern=[[0, 1]], base=N, channel_multiplier=1,
                                  allow_small_or_imprecise_dtypes=True))
        s(pool, lambda: pool.iota(iota_row[:, :], pattern=[[1, P]], base=0, channel_multiplier=0,
                                  allow_small_or_imprecise_dtypes=True))
        s(dve, lambda: dve.memset(XTa[:, :], 0.0))
        s(dve, lambda: dve.memset(X[:, (NB - 1) * D:], 0.0))
        s(dve, lambda: dve.memset(vec[:, :], 0.0))
        s(dve, lambda: dve.memset(small[:, :], 0.0))
        pad_i = btab[0:1, 0:P * TP - E]
        zero_i = btab[0:1, 512:512 + P * TP - E]
        s(dve, lambda: dve.memset(btab[:, :], 0))
        s(dve, lambda: dve.memset(pad_i, PAD_DST))
        flat = lambda t: t.rearrange("t e -> (t e)")
        zeros = XTa[:, 0:D]
        loads = []

        def load(dst, src):
            loads.append((dst, src))

        full = N // P
        load(Xb[:, 0:full, :], a["x"][0:full * P, :].rearrange("(b p) f -> p b f", p=P))
        load(Xb[0:N - full * P, full, :], a["x"][full * P:N, :])
        for pad, name, fill in ((src_pad, "src", zero_i), (dst_pad, "dst", pad_i)):
            load(flat(pad)[0:E].rearrange("(p c) -> p c", p=125), a[name].rearrange("(p c) -> p c", p=125))
            load(row(flat(pad)[E:]), fill)
        load(flat(ea3_pad)[0:3 * E].rearrange("(p c) -> p c", p=125),
             a["edge_attr_3"].rearrange("(p c) k -> p (c k)", p=125))
        n_pad = 3 * (P * TP - E)
        load(row(flat(ea3_pad)[3 * E:]), XTa[0:1, 0:n_pad])
        tail0 = (2 * L1I - 1) * L1U * P
        load(tail_rows[0:E - tail0, :], a["edge_attr_128"][tail0:E, :])
        left = L1U * P - (E - tail0)
        for r in range(0, left, P):
            n = min(P, left - r)
            load(tail_rows[E - tail0 + r:E - tail0 + r + n, :], XTa[0:n, 0:D])
        for t in range(TABLES):
            load(sums[t].rearrange("(b p) f -> p b f", p=P), XTa[:, :].rearrange("p (b f) -> p b f", f=D))
        gat_w = [a["L0_gnn_W"]] + [a[f"L2_gnn_W{l}"] for l in (1, 2, 3)]
        for l in range(4):
            load(Wext[:, l * (D + 2):l * (D + 2) + D], gat_w[l])
        l1w = [a["L1_gnn_W_c"][0:D, :], a["L1_gnn_W_c"][D:2 * D, :], a["L1_gnn_W_c"][2 * D:3 * D, :],
               a["L1_gnn_W1"], a["L1_gnn_W2"], a["L1_gnn_W3"]]
        for i, w in enumerate(l1w):
            load(Wst[:, i * D:(i + 1) * D], w)
        load(vcol("gf"), a["L1_gnn_global_feat"].rearrange("a n -> n a"))
        for v in ("b_c", "b1", "b2", "b3"):
            load(vcol("L1" + v), col(a["L1_gnn_" + v]))
        for l in range(3):
            for v in L2VECS:
                load(vcol(f"L2{v}{l}"), col(a[f"L2_gnn_{v}{l + 1}"]))
        for l in range(GIN):
            for v in GVECS:
                load(vcol(f"G{v}{l}"), col(a["L3_gnn_" + v][l, :]))
        for l, (n1, n2) in enumerate([("L0_gnn_attn_l", "L0_gnn_attn_r")] +
                                     [(f"L2_gnn_as{l}", f"L2_gnn_ad{l}") for l in (1, 2, 3)]):
            load(vcol(f"as{l}"), col(a[n1]))
            load(vcol(f"ad{l}"), col(a[n2]))
        for l in range(3):
            load(vcol(f"ae{l}"), col(a[f"L2_gnn_ae{l + 1}"]))
            for c in range(3):
                load(vcol(f"We{l}{c}"), col(a[f"L2_gnn_We{l + 1}"][c, :]))
        for eng in (sp, act):
            s.wait(eng)
        with nc.allow_non_contiguous_dma(reason="vectors laid along partitions"):
            for i, (dst, src) in enumerate(loads):
                (sp, act)[i % 2].dma_start(dst, src).then_inc(q["load"], 16)
            firsts = XTb[0:1, 0:T].bitcast(I32)
            sp.dma_start(firsts, row(a["dst"][0:1 + (T - 1) * P:P])).then_inc(q["load"], 16)
        for eng in (pe, dve, act, pool, sp):
            eng.wait_ge(q["load"], 16 * (len(loads) + 1))
        end_phase()

        start_row = XTb[0:1, 1024:1024 + TP]
        cmp_out = XTb[:, 2048:2048 + TP]
        kcol = small[:, 0:KJ]
        tcol = small[:, 8:8 + KJ]
        bcol = small[:, 16:16 + KJ]
        b128 = small[:, 24:24 + KJ]
        tcol_i = idx[0][:, 0:1]
        srcR = S[:, 0:KP].bitcast(I32)
        dstR = S[:, KP:2 * KP].bitcast(I32)
        eaR = S[:, 2 * KP:5 * KP]
        dlocR = XTa[:, 0:KP]
        srcF = XTa[:, KP:2 * KP]
        alR = XTa[:, 2 * KP:3 * KP]
        dlocB = XTa[:, 3 * KP:4 * KP].bitcast(BF16)[:, 0:KP]
        srcI = XTa[:, 4 * KP:5 * KP].bitcast(I32)
        s = Serial()
        s(pool, lambda: pool.iota(kcol, pattern=[[P, KJ]], base=0, channel_multiplier=1,
                                  allow_small_or_imprecise_dtypes=True))
        s(pool, lambda: pool.iota(start_row, pattern=[[1, TP]], base=0, channel_multiplier=0,
                                  allow_small_or_imprecise_dtypes=True))
        s(dve, lambda: dve.tensor_scalar(firsts, firsts, 7, None, ALU.logical_shift_right))
        s(dve, lambda: dve.memset(firsts[:, 0:1], 0))
        s(dve, lambda: dve.tensor_copy(XTb[0:1, 3072:3072 + T], firsts))
        s(dve, lambda: dve.tensor_tensor(start_row[:, 0:T], start_row[:, 0:T], XTb[0:1, 3072:3072 + T], ALU.add))
        s(dve, lambda: dve.memset(start_row[:, T:TP], float(T + NB - 1)))
        for o in range(0, TP, 512):
            n = min(512, TP - o)
            s(pe, lambda: pe.matmul(PS[:, o:o + n], ones[0:1, :], start_row[:, o:o + n], start=True, stop=True))
        for j in range(KJ):
            s(dve, lambda: dve.tensor_scalar(cmp_out, PS[:, 0:TP], kcol[:, j:j + 1], 0.0, ALU.is_le, ALU.add,
                                             accum_out=tcol[:, j:j + 1]))
        s(dve, lambda: dve.tensor_scalar(tcol, tcol, 1.0, None, ALU.subtract))
        s(dve, lambda: dve.tensor_tensor(bcol, kcol, tcol, ALU.subtract))
        s(dve, lambda: dve.tensor_scalar(b128, bcol, float(P), None, ALU.mult))
        for j in range(KJ):
            s(dve, lambda: dve.tensor_copy(tcol_i, tcol[:, j:j + 1]))
            for dst, tab, w in ((srcR, src_pad, P), (dstR, dst_pad, P), (eaR, ea3_pad, 3 * P)):
                s(pool, lambda: pool.indirect_dma_start(dst[:, j * w:(j + 1) * w], None, tab[:, :],
                                                        bass.IndirectOffsetOnAxis(tcol_i, 0)), 16)
        s(dve, lambda: dve.tensor_copy(srcF, srcR))
        s(dve, lambda: dve.tensor_copy(dlocR, dstR))
        for j in range(KJ):
            v = dlocR[:, j * P:(j + 1) * P]
            s(dve, lambda: dve.tensor_scalar(v, v, b128[:, j:j + 1], None, ALU.subtract))
        s(dve, lambda: dve.tensor_copy(dlocB, dlocR))
        s(sp, lambda: sp.dma_start(dloc_rows.rearrange("(j p) e -> p j e", p=P),
                                   dlocB.rearrange("p (j e) -> p j e", e=P)), 16)

        def to_cols(src, dst):
            for j in range(KJ):
                s(pe, lambda: pe.transpose(PS[:, 2048 + j * P:2048 + (j + 1) * P], src[:, j * P:(j + 1) * P], ident[:, :]))
            s(dve, lambda: dve.tensor_copy(dst, PS[:, 2048:2048 + KP]))

        to_cols(srcF, srcI)
        with nc.allow_non_contiguous_dma(reason="four sources a partition"):
            s(sp, lambda: sp.dma_start(idx_steps.rearrange("g p c -> p g c"),
                                       srcI[:, 0:K].rearrange("p (g c) -> p g c", c=G)), 16)
        to_cols(dlocR, dloc_cols[:, :])
        s(pe, lambda: pe.transpose(PS[0:KJ, 0:P], bcol, ident[:, :]))
        s(dve, lambda: dve.tensor_copy(rows5[0][0:KJ, 0:P].bitcast(I32), PS[0:KJ, 0:P]))
        s(dve, lambda: dve.memset(btab[:, 0:U], 0))
        s(sp, lambda: sp.dma_start(btab[0:1, U:U + KP].rearrange("a (j p) -> a j p", p=P),
                                   rows5[0][0:KJ, 0:P].bitcast(I32)), 16)
        vl = small[:, 32:41]
        eam = small[:, 41:44]
        tmp3 = small[:, 48:51]
        for l in range(3):
            w0 = VB[f"We{l}0"]
            s(pe, lambda: pe.matmul(PS[:, 3 * l:3 * l + 3], vcol(f"ae{l}").to_broadcast([P, P]),
                                    vec[:, w0:w0 + 3], start=True, stop=True))
        s(dve, lambda: dve.tensor_copy(vl, PS[:, 0:9]))
        ea_all = S[0:125, 0:2550]
        for l in range(3):
            for c in range(3):
                v = eaR.rearrange("p (n c) -> p n c", c=3)[:, :, c]
                w = vl[:, 3 * l + c:3 * l + c + 1]
                if c == 0:
                    s(dve, lambda: dve.tensor_scalar(alR, v, w, None, ALU.mult))
                else:
                    s(dve, lambda: dve.scalar_tensor_tensor(alR, v, w, alR, ALU.mult, ALU.add))
            to_cols(alR, al_cols[:, (l + 1) * KP:(l + 2) * KP])
        s(dve, lambda: dve.memset(al_cols[:, 0:KP], 0.0))
        s(sp, lambda: sp.dma_start(ea_all, a["edge_attr_3"].rearrange("(p c) k -> p (c k)", p=125)), 16)
        s(dve, lambda: dve.tensor_reduce(tmp3[0:125, :], ea_all.rearrange("p (n c) -> p c n", c=3), AX.X, ALU.add))
        s(pe, lambda: pe.matmul(PS[:, 0:3], ones[0:125, :], tmp3[0:125, :], start=True, stop=True))
        s(dve, lambda: dve.tensor_scalar(eam, PS[:, 0:3], 1.0 / E, None, ALU.mult))
        for l in range(3):
            s(dve, lambda: dve.tensor_tensor(tmp3, eam, vl[:, 3 * l:3 * l + 3], ALU.mult))
            s(dve, lambda: dve.tensor_reduce(aloop[:, l:l + 1], tmp3, AX.X, ALU.add))
        for l in range(4):
            o = l * (D + 2)
            v0 = VB[f"as{l}"]
            s(pe, lambda: pe.transpose(PS[:, 0:D], Wext[:, o:o + D], ident[:, :]))
            s(dve, lambda: dve.tensor_copy(rows5[0][:, 0:D], PS[:, 0:D]))
            s(pe, lambda: pe.matmul(PS[:, 0:2], rows5[0][:, 0:D], vec[:, v0:v0 + 2], start=True, stop=True))
            s(dve, lambda: dve.tensor_copy(Wext[:, o + D:o + D + 2], PS[:, 0:2]))
        c1 = vcol("c1")
        s(pe, lambda: pe.matmul(PS[:, 0:1], Wst[:, 2 * D:3 * D], vcol("gf"), start=True, stop=True))
        s(dve, lambda: dve.tensor_tensor(c1, PS[:, 0:1], vcol("L1b_c"), ALU.add))
        end_phase([("load2", s.counts["load2"])])

        def group_src(t, c):
            def at(g):
                return t[:, bass.ds(g * (GB * c), GB * c)].rearrange("p (b c) -> p b c", c=c)[:, :, 0:D]
            return at

        HALF = NBP // (2 * GB)

        def turn():
            with pe.Fori(0, HALF) as it:
                for h in range(2):
                    pe.wait_ge(q["stage"], it * 2 + h + 1)
                    pe.wait_ge(q["evac"], it * 2 + h + 1)
                    for u in range(GB):
                        pe.transpose(PS[:, h * 1024 + u * D:h * 1024 + (u + 1) * D],
                                     rows5[h][:, u * D:(u + 1) * D], ident[:, :]).then_inc(q["mm"], 1)

        def node_to_feature(t, c, dst):
            src = group_src(t, c)
            pe.sem_inc(q["mm"], 2 * GB)
            dve.sem_inc(q["evac"], 2)
            with act.Fori(0, HALF) as it:
                for h in range(2):
                    act.wait_ge(q["mm"], it * (2 * GB) + (h + 1) * GB)
                    act.activation(rows5[h][:, :].rearrange("p (b c) -> p b c", c=D), src(it * 2 + h),
                                   ACT.Copy).then_inc(q["stage"], 1)
            turn()
            with dve.Fori(0, HALF) as it:
                for h in range(2):
                    dve.wait_ge(q["mm"], it * (2 * GB) + (h + 3) * GB)
                    dve.tensor_copy(dst[:, bass.ds((it * 2 + h) * (GB * P), GB * P)],
                                    PS[:, h * 1024:h * 1024 + GB * P]).then_inc(q["evac"], 1)
            end_phase()

        def feature_to_node(src, t, c, func, scale, shift, rows=None):
            pe.sem_inc(q["mm"], 2 * GB)
            dve.sem_inc(q["evac"], 2)
            with act.Fori(0, HALF) as it:
                for h in range(2):
                    act.wait_ge(q["mm"], it * (2 * GB) + (h + 1) * GB)
                    act.activation(rows5[h][:, :], src[:, bass.ds((it * 2 + h) * (GB * P), GB * P)],
                                   func, bias=shift, scale=scale).then_inc(q["stage"], 1)
            turn()
            with dve.Fori(0, HALF) as it:
                for h in range(2):
                    dve.wait_ge(q["mm"], it * (2 * GB) + (h + 3) * GB)
                    dve.tensor_copy(group_src(t, c)(it * 2 + h),
                                    PS[:, h * 1024:h * 1024 + GB * P].rearrange("p (b c) -> p b c", c=D)
                                    ).then_inc(q["evac"], 1)
            if rows is not None:
                store_rows(t, c, rows)
            end_phase()

        def store_rows(t, c, rows):
            sp.wait_ge(q["evac"], 2 + 2 * HALF)
            sp.dma_start(rows.rearrange("(b p) f -> p b f", p=P), xb(t, c)[:, :, 0:D]).then_inc(q["out"], 16)
            sp.wait_ge(q["out"], 16)

        def linear(src, w, dst, bias, func=None, scale=None, shift=None, second=None):
            if func is not None:
                with act.Fori(0, NCH // 2) as it:
                    for h in range(2):
                        act.wait_ge(q["mm"], it * 2 + h + 1)
                        act.activation(rows5[h][:, 0:CH], src[:, bass.ds((it * 2 + h) * CH, CH)], func,
                                       bias=shift, scale=scale).then_inc(q["stage"], 1)
            pe.sem_inc(q["mm"], 2)
            dve.sem_inc(q["evac"], 2)
            with pe.Fori(0, NCH // 2) as it:
                for h in range(2):
                    pe.wait_ge(q["evac"], it * 2 + h + 1)
                    if func is not None:
                        pe.wait_ge(q["stage"], it * 2 + h + 1)
                        v = rows5[h][:, 0:CH]
                    else:
                        v = src[:, bass.ds((it * 2 + h) * CH, CH)]
                    m = pe.matmul(bank(h, CH), w, v, start=True, stop=second is None)
                    if second is not None:
                        m = pe.matmul(bank(h, CH), second[1], second[0][:, bass.ds((it * 2 + h) * CH, CH)],
                                      start=False, stop=True)
                    m.then_inc(q["mm"], 1)
            with dve.Fori(0, NCH // 2) as it:
                for h in range(2):
                    dve.wait_ge(q["mm"], it * 2 + h + 3)
                    dve.tensor_scalar(dst[:, bass.ds((it * 2 + h) * CH, CH)], bank(h, CH), bias, None,
                                      ALU.add).then_inc(q["evac"], 1)
            end_phase()

        def norm_stats(src, gamma, beta, relu=False):
            s = Serial()
            if relu:
                s(act, lambda: act.activation(src[:, :], src[:, :], ACT.Relu, bias=aff[:, 1:2], scale=aff[:, 0:1]))
            n = -(-N // 512)
            for i in range(n):
                s(dve, lambda: dve.bn_stats(stat[:, 6 * i:6 * i + 6], src[:, 512 * i:min(512 * i + 512, N)]))
            s(dve, lambda: dve.bn_aggr(small[:, 0:2], stat[:, 0:6 * n]))
            s(dve, lambda: dve.tensor_scalar(small[:, 2:3], small[:, 1:2], EPS, None, ALU.add))
            s(act, lambda: act.activation(small[:, 3:4], small[:, 2:3], ACT.Sqrt))
            s(dve, lambda: dve.reciprocal(small[:, 4:5], small[:, 3:4]))
            s(dve, lambda: dve.tensor_tensor(aff[:, 0:1], small[:, 4:5], gamma, ALU.mult))
            s(dve, lambda: dve.tensor_tensor(small[:, 5:6], small[:, 0:1], aff[:, 0:1], ALU.mult))
            s(dve, lambda: dve.tensor_tensor(aff[:, 1:2], beta, small[:, 5:6], ALU.subtract))
            end_phase()

        def layer_norm():
            s = Serial()
            mean = XTa[:, 0:NBP]
            var = XTa[:, NBP:2 * NBP]
            sq = XTb[:, :]
            bc = lambda t: t.rearrange("p (b a) -> p b a", a=1).to_broadcast([P, NBP, D])
            s(dve, lambda: dve.tensor_tensor(Xb, Xb, Sb[:, :, 0:D], ALU.add))
            s(dve, lambda: dve.tensor_reduce(mean, Xb, AX.X, ALU.add))
            s(dve, lambda: dve.tensor_scalar(mean, mean, 1.0 / D, None, ALU.mult))
            s(dve, lambda: dve.tensor_tensor(Xb, Xb, bc(mean), ALU.subtract))
            s(act, lambda: act.activation(sq, X[:, :], ACT.Square))
            s(dve, lambda: dve.tensor_reduce(var, xb(XTb), AX.X, ALU.add))
            s(dve, lambda: dve.tensor_scalar(var, var, 1.0 / D, EPS, ALU.mult, ALU.add))
            s(act, lambda: act.activation(mean, var, ACT.Sqrt))
            s(dve, lambda: dve.reciprocal(var, mean))
            s(dve, lambda: dve.tensor_tensor(Xb, Xb, bc(var), ALU.mult))
            end_phase()

        def project(l, keep):
            if not keep:
                dve.memset(S[:, :], 0.0).then_inc(q["memset"], 1)
                dve.wait_ge(q["memset"], 1)
                dve.memset(Sb[:, :, MAX], BIG).then_inc(q["memset"], 1)
            else:
                dve.memset(Sb[:, :, DEN], 1.0).then_inc(q["memset"], 1)
            W2 = D + 2
            pe.sem_inc(q["mm"], 2)
            dve.sem_inc(q["evac"], 2)
            act.sem_inc(q["out"], 4)
            for h in range(2):
                sp.sem_inc(q[f"st{h}"], 16)
            with act.Fori(0, HALF) as it:
                for h in range(2):
                    act.wait_ge(q["mm"], it * 2 + h + 1)
                    act.activation(rows5[h][:, :], XTa[:, bass.ds((it * 2 + h) * (GB * P), GB * P)],
                                   ACT.Identity, bias=aff[:, 1:2], scale=aff[:, 0:1]).then_inc(q["stage"], 1)
                    act.wait_ge(q["mm"], it * 2 + h + 3)
                    act.wait_ge(q[f"st{h}"], it * 16 + 16)
                    for b0, n in ((0, 3), (3, GB - 3)):
                        v = PS[:, h * 1024 + b0 // 3 * 512:h * 1024 + b0 // 3 * 512 + n * W2]
                        act.activation(gst[h][:, b0 * R:(b0 + n) * R].rearrange("p (b c) -> p b c", c=R),
                                       v.rearrange("p (b c) -> p b c", c=W2)[:, :, 0:R], ACT.Copy
                                       ).then_inc(q["out"], 1)
            with pe.Fori(0, HALF) as it:
                for h in range(2):
                    pe.wait_ge(q["stage"], it * 2 + h + 1)
                    pe.wait_ge(q["evac"], it * 2 + h + 1)
                    for u in range(GB):
                        o = h * 1024 + u // 3 * 512 + u % 3 * W2
                        m = pe.matmul(PS[:, o:o + W2], rows5[h][:, u * P:(u + 1) * P],
                                      Wcur[:, :], start=True, stop=True)
                    m.then_inc(q["mm"], 1)
            dve.wait_ge(q["memset"], 1 if keep else 2)
            with dve.Fori(0, HALF) as it:
                for h in range(2):
                    dve.wait_ge(q["out"], (it * 2 + h) * 2 + 6)
                    for b0, n in ((0, 3), (3, GB - 3)):
                        o = h * 1024 + b0 // 3 * 512
                        v = PS[:, o:o + n * W2].rearrange("p (b c) -> p b c", c=W2)
                        st = S[:, bass.ds((it * 2 + h) * (GB * C) + b0 * C, n * C)] \
                            .rearrange("p (b c) -> p b c", c=C)
                        if keep:
                            dve.tensor_copy(st[:, :, 0:D], v[:, :, 0:D])
                            dve.tensor_scalar(st[:, :, MAX:MAX + 1], v[:, :, D:D + 1], cur[:, 3:4], None, ALU.add)
                        last = dve.tensor_copy(st[:, :, ER:ER + 1], v[:, :, D + 1:D + 2])
                    last.then_inc(q["evac"], 1)
            with sp.Fori(0, HALF) as it:
                for h in range(2):
                    sp.wait_ge(q["out"], (it * 2 + h) * 2 + 6)
                    sp.dma_start(gat_rows[bass.ds((it * 2 + h) * (GB * P), GB * P), :]
                                 .rearrange("(b p) f -> p b f", p=P),
                                 gst[h][:, :].rearrange("p (b c) -> p b c", c=R)).then_inc(q[f"st{h}"], 16)
            for h in range(2):
                sp.wait_ge(q[f"st{h}"], 16 * HALF + 16)
            end_phase()

        Wcur = sb("w_cur", D + 2)
        cur = sb("cur", 4)
        def fetch(table, width):
            def sp_part(it, first):
                for g in range(NG):
                    if not first:
                        sp.wait_ge(q[f"rows{g}"], it * (16 * G))
                    sp.dma_start(idx[g][:, :], idx_steps[bass.ds(it * NG + g, 1), :, :]
                                 .rearrange("a p c -> (a p) c")).then_inc(q[f"idx{g}"], 16)
                    if width == R:
                        sp.wait_ge(q["m_ready"], it * NG + g + 1)
                        sp.dma_start(dl[g][:, :], dloc_rows[bass.ds(it * U + g * G, G), :]
                                     .rearrange("(a s) e -> a (s e)", a=1).to_broadcast([P, G * P])
                                     ).then_inc(q[f"dl{g}"], 16)

            sp_part(0, True)
            with sp.Fori(1, ITER) as it:
                sp_part(it, False)
            if width == R:
                dve.sem_inc(q["m_ready"], NG)
            pe.sem_inc(q["product"], U)
            with pool.Fori(0, ITER) as it:
                for g in range(NG):
                    pool.wait_ge(q[f"idx{g}"], it * 16 + 16)
                    pool.wait_ge(q["product"], it * U + (g + 1) * G)
                    settled(pool)
                    for u in range(G):
                        pool.indirect_dma_start(grow[g][:, u * R:u * R + width], None, table[:, :],
                                                bass.IndirectOffsetOnAxis(idx[g][:, u:u + 1], 0)
                                                ).then_inc(q[f"rows{g}"], 16)

        BS, BP, BO = 0, 2, 4

        def gat_edges(al0):
            fetch(gat_rows, R)

            def run(eng, body, lag, lead):
                def part(base, gbase, us, has):
                    bn = None
                    if lead is not None:
                        first = 0 if (isinstance(base, int) and base == 0) else -lead
                        last = U if has else 0
                        bn = {i: eng.value_load(btab[0:1, bass.ds(base + (U + i), 1)], min_val=0, max_val=NB - 1)
                              for i in range(first, last)}
                    for u in us:
                        body(base, gbase, u, (lambda d, u=u: (has or d > u) and
                                              (not (isinstance(base, int) and base == 0) or u >= d)), bn)
                part(0, 0, range(U), True)
                with eng.Fori(1, ITER) as it:
                    part(it * U, it * NG, range(U), True)
                part(K, ITER * NG, range(lag), False)

            def pe_body(base, gbase, u, live, bn):
                n = base + u
                if live(0):
                    g = u // G
                    if u % G == 0:
                        pe.wait_ge(q["s_ready"], gbase + g + 1)
                    if live(2):
                        pe.wait_ge(q["masked"], n - 1)
                    pe.matmul(bank(BS + u % 2, P), s_col[g][:, u % G:u % G + 1].to_broadcast([P, P]),
                              ident[:, :], start=True, stop=True).then_inc(q["bcast"], 1)
                if live(2):
                    v = (u - 2) % U
                    pe.wait_ge(q["weights"], n - 1)
                    if live(4):
                        pe.wait_ge(q["pw_ready"], n - 3)
                    pe.transpose(bank(BP + v % 2, P), pt[v % 8][:, 0:P], ident[:, :]
                                 ).then_inc(q["transposed"], 1)
                if live(4):
                    v = (u - 4) % U
                    pe.wait_ge(q["pw_ready"], n - 3)
                    if live(6):
                        pe.wait_ge(q["summed"], n - 5)
                    pe.matmul(bank(BO + v % 2, R), pw[v % 4][:, :],
                              grow[v // G][:, v % G * R:(v % G + 1) * R],
                              start=True, stop=True).then_inc(q["product"], 1)

            def dve_body(base, gbase, u, live, bn):
                n = base + u
                if live(0):
                    g = u // G
                    if u % G == 0:
                        rows = grow[g][:, :].rearrange("p (s c) -> p s c", c=R)[:, :, D]
                        dve.wait_ge(q[f"rows{g}"], gbase * (16 * G // NG) + 16 * G)
                        if live(U):
                            dve.wait_ge(q["bcast"], n - (U - G))
                        dve.tensor_tensor(s_col[g][:, :], rows, al_cols[:, bass.ds(n + al0, G)],
                                          ALU.add).then_inc(q["s_ready"], 1)
                        dve.wait_ge(q["s_ready"], gbase + g + 1)
                        dve.memset(rows, 1.0)
                        dve.wait_ge(q[f"dl{g}"], gbase * (16 // NG) + 16)
                        dve.tensor_scalar(mask[g][:, :], dl[g][:, :], iota_p[:, :], BIG, ALU.not_equal,
                                          ALU.mult).then_inc(q["m_ready"], 1)
                        dve.wait_ge(q["m_ready"], gbase + g + 1 + NG)
                    b = bn[u]
                    m = sm[u % 4]
                    if live(4):
                        dve.wait_ge(q["act_a"], n - 3)
                    if live(1):
                        dve.wait_ge(q["new_max"], n)
                    dve.tensor_scalar(m[:, P + 1:P + 2], S[:, bass.ds(b * C + MAX, 1)], 1.0, None, ALU.mult
                                      ).then_inc(q["old_max"], 1)
                if live(1):
                    w = um[(u - 1) % 2]
                    dve.wait_ge(q["act_a"], n)
                    dve.scalar_tensor_tensor(w[:, :], w[:, :], 0.2, w[:, :], ALU.mult, ALU.max
                                             ).then_inc(q["leaky"], 1)
                    dve.wait_ge(q["leaky"], n)
                    if live(3):
                        dve.wait_ge(q["weights"], n - 2)
                    dve.tensor_scalar(neg[(u - 1) % 2][:, :], w[:, P:P + 1], -1.0, None, ALU.mult
                                      ).then_inc(q["act_b"], 1)
                if live(0):
                    dve.wait_ge(q["bcast"], n + 1)
                    dve.wait_ge(q["old_max"], n + 1)
                    settled(dve)
                    dve.tensor_tensor_reduce(out=m[:, 0:P], in0=bank(BS + u % 2, P),
                                             in1=mask[g][:, u % G * P:(u % G + 1) * P], scale=1.0,
                                             scalar=m[:, P + 1:P + 2], op0=ALU.add, op1=ALU.max,
                                             accum_out=m[:, P:P + 1]).then_inc(q["masked"], 1)
                if live(5):
                    v = (u - 5) % U
                    st = S[:, bass.ds(bn[u - 5] * C, R)]
                    dve.wait_ge(q["product"], n - 4 + U)
                    if live(6):
                        dve.wait_ge(q["summed"], n - 5)
                    dve.scalar_tensor_tensor(st, st, pt[v % 8][:, P + 1:P + 2], bank(BO + v % 2, R),
                                             ALU.mult, ALU.add).then_inc(q["summed"], 1)
                if live(0):
                    dve.wait_ge(q["masked"], n + 1)
                    dve.tensor_scalar(S[:, bass.ds(b * C + MAX, 1)], m[:, P:P + 1], 1.0, None, ALU.mult
                                      ).then_inc(q["new_max"], 1)

            def act_body(base, gbase, u, live, bn):
                n = base + u
                if live(1):
                    v = (u - 1) % U
                    act.wait_ge(q["act_b"], n)
                    if live(9):
                        act.wait_ge(q["summed"], n - 8)
                    act.activation(pt[v % 8][:, :], um[v % 2][:, :], ACT.Exp, bias=neg[v % 2][:, :]
                                   ).then_inc(q["weights"], 1)
                if live(3):
                    v = (u - 3) % U
                    act.wait_ge(q["transposed"], n - 2)
                    if live(7):
                        act.wait_ge(q["product"], n - 6 + U)
                    act.activation(pw[v % 4][:, :], bank(BP + v % 2, P), ACT.Copy).then_inc(q["pw_ready"], 1)
                if live(0):
                    act.wait_ge(q["masked"], n + 1)
                    if live(2):
                        act.wait_ge(q["weights"], n - 1)
                    act.activation(um[u % 2][:, :], sm[u % 4][:, :], ACT.Identity,
                                   bias=S[:, bass.ds(bn[u] * C + ER, 1)]).then_inc(q["act_a"], 1)

            run(pe, pe_body, 4, None)
            run(dve, dve_body, 5, 5)
            run(act, act_body, 3, 0)
            end_phase([(f"rows{g}", ITER * G * 16) for g in range(NG)])

        def gin_edges():
            fetch(gin_rows, D)

            def run(eng, body, lag, lead):
                def part(base, gbase, us, has):
                    first = 0 if (isinstance(base, int) and base == 0) else -lead
                    bn = None
                    if lead:
                        bn = {i: eng.value_load(btab[0:1, bass.ds(base + (U + i), 1)], min_val=0, max_val=NB - 1)
                              for i in range(first, U - lead if has else 0)}
                    for u in us:
                        body(base, gbase, u, (lambda d, u=u: (has or d > u) and
                                              (not (isinstance(base, int) and base == 0) or u >= d)), bn)
                part(0, 0, range(U), True)
                with eng.Fori(1, ITER) as it:
                    part(it * U, it * NG, range(U), True)
                part(K, ITER * NG, range(lag), False)

            def pe_body(base, gbase, u, live, bn):
                n = base + u
                g = u // G
                if u % G == 0:
                    pe.wait_ge(q[f"rows{g}"], gbase * (16 * G // NG) + 16 * G)
                pe.wait_ge(q["eq"], n + 1)
                if live(4):
                    pe.wait_ge(q["summed"], n - 3)
                pe.matmul(bank(u % 4, D), pw[u % 4][:, :], grow[g][:, u % G * R:u % G * R + D],
                          start=True, stop=True).then_inc(q["product"], 1)

            def dve_body(base, gbase, u, live, bn):
                n = base + u
                if live(0):
                    if live(4):
                        dve.wait_ge(q["product"], n - 3 + U)
                    dve.tensor_scalar(pw[u % 4][:, :], iota_row[:, :], dloc_cols[:, bass.ds(n, 1)], None,
                                      ALU.is_equal).then_inc(q["eq"], 1)
                if live(2):
                    v = (u - 2) % U
                    st = S[:, bass.ds(bn[u - 2] * C, D)]
                    dve.wait_ge(q["product"], n - 1 + U)
                    if live(3):
                        dve.wait_ge(q["summed"], n - 2)
                    dve.tensor_tensor(st, st, bank(v % 4, D), ALU.add).then_inc(q["summed"], 1)

            run(pe, pe_body, 0, 0)
            run(dve, dve_body, 2, 2)
            end_phase([(f"rows{g}", ITER * G * 16) for g in range(NG)])

        def edge_sums():
            src_c = XTb[:, 0:2 * L1I * L1U]
            s = Serial()
            si = XTa[:, 0:KP].bitcast(I32)
            sf = XTa[:, KP:2 * KP]
            nj = -(-TP // P)
            s(dve, lambda: dve.memset(XTa[:, 0:2 * KP], 0.0))
            for j in range(nj):
                n = min(P, TP - j * P)
                s(sp, lambda: sp.dma_start(si[0:n, j * P:(j + 1) * P], src_pad[j * P:j * P + n, :]), 16)
            s(dve, lambda: dve.tensor_copy(sf, si))
            for j in range(nj):
                s(pe, lambda: pe.transpose(PS[:, j * P:(j + 1) * P], sf[:, j * P:(j + 1) * P], ident[:, :]))
            s(dve, lambda: dve.tensor_copy(src_c, PS[:, 0:2 * L1I * L1U]))
            end_phase()
            ea = [XTa[:, i * 1024:(i + 1) * 1024] for i in range(2)]
            vals = [XTa[:, 2048 + i * P:2048 + (i + 1) * P] for i in range(2 * L1U)]
            eqs = [XTb[:, 1024 + i * P:1024 + (i + 1) * P] for i in range(4)]
            junk = XTb[:, 2048:2048 + P]
            cnt = [small[:, 8 * h:8 * h + 8] for h in range(2)]
            fl = small[:, 16:24]
            to = small[:, 24:32]
            ix = [small[:, 32 + 8 * h:40 + 8 * h].bitcast(I32) for h in range(2)]
            per = 2 * L1U
            rows_of = a["edge_attr_128"]

            def ld(it, h, src):
                sp.wait_ge(q["product"], it * per + h * L1U + L1U)
                sp.dma_start(ea[h].rearrange("p (t f) -> p t f", f=D), src).then_inc(q[f"ld{h}"], 16)

            pe.sem_inc(q["product"], per)
            tile_rows = lambda v: v.rearrange("(t p) f -> p t f", p=P)
            with sp.Fori(0, L1I - 1) as it:
                for h in range(2):
                    ld(it, h, tile_rows(rows_of[bass.ds((it * 2 + h) * (L1U * P), L1U * P), :]))
            ld(L1I - 1, 0, tile_rows(rows_of[(L1I - 1) * 2 * L1U * P:((L1I - 1) * 2 + 1) * L1U * P, :]))
            ld(L1I - 1, 1, tile_rows(tail_rows))
            act.sem_inc(q["evac"], 4)

            def pe_part(it, first):
                for u in range(per):
                    h = u // L1U
                    pe.wait_ge(q["s_ready"], it * 2 + h + 1)
                    if not (first and u < 2):
                        pe.wait_ge(q["eq"], it * per + u - 1)
                    pe.matmul(bank(u % 2, P), colst[h][:, u % L1U:u % L1U + 1].to_broadcast([P, P]), ident[:, :],
                              start=True, stop=True).then_inc(q["bcast"], 1)
                    if not (first and u < 1):
                        prod(it, u - 1, first and u - 1 < 4)

            def prod(it, u, fresh):
                h = (u % per) // L1U
                n = it * per + u
                if u % L1U == 0:
                    pe.wait_ge(q[f"ld{h}"], it * 16 + 16 if u >= 0 else it * 16)
                pe.wait_ge(q["eq"], n + 1)
                pe.wait_ge(q["evac"], n + 1)
                pe.matmul(bank(2 + u % 4, P), eqs[u % 4], ea[h][:, u % L1U * D:(u % L1U + 1) * D],
                          start=True, stop=True).then_inc(q["product"], 1)

            pe_part(0, True)
            with pe.Fori(1, L1I) as it:
                pe_part(it, False)
            prod(L1I, -1, False)

            def dve_part(it, first):
                for h in range(2):
                    c = colst[h]
                    if not first:
                        dve.wait_ge(q["bcast"], it * per - per + (h + 1) * L1U)
                    dve.tensor_copy(c[:, :], src_c[:, bass.ds((it * 2 + h) * L1U, L1U)]
                                    if not first else src_c[:, h * L1U:(h + 1) * L1U]).then_inc(q["s_ready"], 1)
                    dve.wait_ge(q["s_ready"], it * 2 + h + 1)
                    for u in range(L1U):
                        n = it * per + h * L1U + u
                        k = h * L1U + u
                        dve.wait_ge(q["bcast"], n + 1)
                        if not (first and k < 4):
                            dve.wait_ge(q["product"], n - 3 + per)
                        dve.tensor_scalar(eqs[k % 4], bank(k % 2, P), c[:, u:u + 1], None, ALU.is_equal
                                          ).then_inc(q["eq"], 1)
                        dve.wait_ge(q["eq"], n + 1)
                        settled(dve)
                        dve.tensor_tensor_reduce(out=junk, in0=eqs[k % 4], in1=lower[:, :], scale=1.0, scalar=0.0,
                                                 op0=ALU.mult, op1=ALU.add, accum_out=cnt[h][:, u:u + 1]
                                                 ).then_inc(q["first"], 1)
                    g0 = it * 2 + h
                    dve.wait_ge(q["first"], it * per + (h + 1) * L1U)
                    dve.tensor_scalar(fl, cnt[h], 0.5, None, ALU.is_gt).then_inc(q["act_a"], 1)
                    dve.tensor_scalar(to, c[:, :], dump[:, :], -1.0, ALU.subtract, ALU.mult).then_inc(q["act_a"], 1)
                    dve.wait_ge(q["act_a"], g0 * 4 + 2)
                    dve.tensor_tensor(to, to, fl, ALU.mult).then_inc(q["act_a"], 1)
                    dve.wait_ge(q["act_a"], g0 * 4 + 3)
                    dve.tensor_tensor(to, to, c[:, :], ALU.add).then_inc(q["act_a"], 1)
                    dve.wait_ge(q["act_a"], g0 * 4 + 4)
                    if not first:
                        for t in range(TABLES):
                            dve.wait_ge(q[f"tab{t}"], it * (16 * per // TABLES) - (1 - h) * (16 * L1U // TABLES))
                    dve.tensor_copy(ix[h], to).then_inc(q["index"], 1)

            dve_part(0, True)
            with dve.Fori(1, L1I) as it:
                dve_part(it, False)

            def act_part(it, first):
                for u in range(per):
                    n = it * per + u
                    act.wait_ge(q["product"], n + 1 + per)
                    if not first:
                        act.wait_ge(q[f"tab{u % TABLES}"], it * (16 * per // TABLES) - 16 * (per // TABLES - 1 - u // TABLES))
                    act.activation(vals[u], bank(2 + u % 4, P), ACT.Copy).then_inc(q["evac"], 1)

            act_part(0, True)
            with act.Fori(1, L1I) as it:
                act_part(it, False)

            def pool_part(it, first):
                for u in range(per):
                    h = u // L1U
                    t = u % TABLES
                    pool.wait_ge(q["index"], it * 2 + h + 1)
                    pool.wait_ge(q["evac"], it * per + u + 1 + 4)
                    if not (first and u < TABLES):
                        pool.wait_ge(q[f"tab{t}"], it * (16 * per // TABLES) + 16 * (u // TABLES))
                    settled(pool)
                    pool.indirect_dma_start(sums[t][:, :], bass.IndirectOffsetOnAxis(ix[h][:, u % L1U:u % L1U + 1], 0),
                                            vals[u], None, compute_op=ALU.add).then_inc(q[f"tab{t}"], 16)

            pool_part(0, True)
            with pool.Fori(1, L1I) as it:
                pool_part(it, False)
            end_phase([(f"tab{t}", L1I * per // TABLES * 16) for t in range(TABLES)])


        s = Serial()
        s(dve, lambda: dve.memset(aff[:, 0:1], 1.0))
        s(dve, lambda: dve.memset(aff[:, 1:2], 0.0))
        s(dve, lambda: dve.tensor_copy(Wcur[:, :], Wext[:, 0:D + 2]))
        end_phase()
        node_to_feature(X, D, XTa)
        project(0, False)
        gat_edges(0)

        def divide_state(floor, has):
            s = Serial()
            den = XTb[:, 0:NBP]
            flag = XTb[:, NBP:2 * NBP]
            s(dve, lambda: dve.tensor_scalar(den, Sb[:, :, DEN], floor[1], None, floor[0]))
            s(dve, lambda: dve.reciprocal(den, den))
            if has:
                s(dve, lambda: dve.tensor_scalar(flag, Sb[:, :, MAX], BIG / 2, None, ALU.is_gt))
                s(dve, lambda: dve.tensor_tensor(den, den, flag, ALU.mult))
            s(dve, lambda: dve.tensor_tensor(Sb[:, :, 0:D], Sb[:, :, 0:D],
                                             den.rearrange("p (b a) -> p b a", a=1).to_broadcast([P, NBP, D]),
                                             ALU.mult))
            end_phase()

        divide_state((ALU.max, 1e-9), True)
        layer_norm()

        edge_sums()
        s = Serial()
        tab = lambda t: sums[t].rearrange("(b p) f -> p b f", p=P)
        s(sp, lambda: sp.dma_start(Sb[:, :, 0:D], tab(0)), 16)
        s(sp, lambda: sp.dma_start(xb(XTa), tab(1)), 16)
        s(sp, lambda: sp.dma_start(xb(XTb), tab(2)), 16)
        s(dve, lambda: dve.tensor_tensor(Sb[:, :, 0:D], Sb[:, :, 0:D], xb(XTa), ALU.add))
        s(sp, lambda: sp.dma_start(xb(XTa), tab(3)), 16)
        s(dve, lambda: dve.tensor_tensor(xb(XTb), xb(XTb), xb(XTa), ALU.add))
        s(dve, lambda: dve.tensor_tensor(Sb[:, :, 0:D], Sb[:, :, 0:D], xb(XTb), ALU.add))
        end_phase()
        node_to_feature(X, D, XTa)
        node_to_feature(S, C, XTb)
        wst = lambda i: Wst[:, i * D:(i + 1) * D]

        def softplus(t):
            s = Serial()
            tmp = S[:, 0:NP]
            s(act, lambda: act.activation(tmp, t[:, :], ACT.Abs))
            s(act, lambda: act.activation(tmp, tmp, ACT.Exp, scale=-1.0))
            s(act, lambda: act.activation(tmp, tmp, ACT.Ln, bias=1.0))
            s(dve, lambda: dve.scalar_tensor_tensor(t[:, :], t[:, :], 0.0, tmp, ALU.max, ALU.add))
            end_phase()

        linear(XTa, wst(0), S, c1, second=(XTb, wst(1)))
        linear(S, wst(3), XTb, vcol("L1b1"))
        softplus(XTb)
        linear(XTb, wst(4), XTa, vcol("L1b2"))
        softplus(XTa)
        linear(XTa, wst(5), XTb, vcol("L1b3"))
        feature_to_node(XTb, S, C, ACT.Copy, 1.0, 0.0)
        layer_norm()

        node_to_feature(X, D, XTa)
        with nc.Fori(0, 3) as l:
            s = Serial()
            s(dve, lambda: dve.tensor_copy(Wcur[:, :], Wext[:, bass.ds(l * (D + 2) + (D + 2), D + 2)]))
            s(dve, lambda: dve.tensor_copy(cur[:, 0:3], vec[:, bass.ds(l * 3 + VB["L2b0"], 3)]))
            s(dve, lambda: dve.tensor_copy(cur[:, 3:4], aloop[:, bass.ds(l, 1)]))
            end_phase()
            project(l, True)
            gat_edges(l * KP + KP)
            divide_state((ALU.add, 1e-16), False)
            node_to_feature(S, C, XTa)
            s = Serial()
            s(dve, lambda: dve.tensor_scalar(XTa[:, :], XTa[:, :], cur[:, 0:1], None, ALU.add))
            s(dve, lambda: dve.scalar_tensor_tensor(XTa[:, :], XTa[:, :], 0.01, XTa[:, :], ALU.mult, ALU.max))
            end_phase()
            norm_stats(XTa, cur[:, 1:2], cur[:, 2:3])
        feature_to_node(XTa, S, C, ACT.Identity, aff[:, 0:1], aff[:, 1:2])
        layer_norm()

        s = Serial()
        s(dve, lambda: dve.tensor_copy(Sb[:, :, 0:D], Xb))
        s(sp, lambda: sp.dma_start(gin_rows.rearrange("(b p) f -> p b f", p=P), Xb), 16)
        s.wait(sp)
        end_phase()
        gcur = sb("gin_cur", len(GVECS))
        gv = {v: gcur[:, i:i + 1] for i, v in enumerate(GVECS)}
        with nc.Fori(0, GIN) as l:
            s = Serial()
            for i, name in enumerate(("L3_gnn_W1", "L3_gnn_W2")):
                s(sp, lambda: sp.dma_start(wst(6 + i), a[name][bass.ds(l, 1), :, :]
                                           .rearrange("a i o -> (a i) o")), 16)
            s(dve, lambda: dve.tensor_copy(gcur[:, :], vec[:, bass.ds(l * len(GVECS) + VB["Gb10"], len(GVECS))]))
            end_phase()
            gin_edges()
            node_to_feature(S, C, XTa)
            linear(XTa, wst(6), XTb, gv["b1"])
            norm_stats(XTb, gv["bn1_g"], gv["bn1_b"])
            linear(XTb, wst(7), XTa, gv["b2"], ACT.Relu, aff[:, 0:1], aff[:, 1:2])
            norm_stats(XTa, gv["bn2_g"], gv["bn2_b"])
            norm_stats(XTa, gv["bn3_g"], gv["bn3_b"], relu=True)
            feature_to_node(XTa, S, C, ACT.Relu, aff[:, 0:1], aff[:, 1:2], gin_rows)
        layer_norm()
        sp.dma_start(out[0:full * P, :].rearrange("(b p) f -> p b f", p=P), Xb[:, 0:full, :]).then_inc(q["out"], 16)
        sp.dma_start(out[full * P:N, :], Xb[0:N - full * P, full, :]).then_inc(q["out"], 16)
        sp.wait_ge(q["out"], 32)


INS = ["x", "src", "dst", "edge_attr_128", "edge_attr_3", "L0_gnn_W", "L0_gnn_attn_l", "L0_gnn_attn_r",
       "L1_gnn_global_feat", "L1_gnn_W_c", "L1_gnn_b_c", "L1_gnn_W1", "L1_gnn_b1", "L1_gnn_W2", "L1_gnn_b2",
       "L1_gnn_W3", "L1_gnn_b3"] + \
      [f"L2_gnn_{v}{l}" for l in (1, 2, 3) for v in ("W", "as", "ad", "We", "ae", "b", "g", "be")] + \
      ["L3_gnn_W1", "L3_gnn_W2"] + ["L3_gnn_" + v for v in GVECS]


def kernel(**inputs):
    import numpy as np
    import concourse.bacc as bacc
    from concourse.bass_utils import run_bass_kernel_spmd

    nc = bacc.Bacc("TRN2", target_bir_lowering=False, num_devices=1)
    arrays, aps = {}, {}
    for name in INS:
        v = np.ascontiguousarray(inputs[name])
        arrays["in_" + name] = v
        aps[name] = nc.dram_tensor("in_" + name, v.shape, mybir.dt.from_np(v.dtype), kind="ExternalInput").ap()
    out = nc.dram_tensor("out_0", (N, D), F32, kind="ExternalOutput").ap()
    build(nc, aps, out)
    r = run_bass_kernel_spmd(nc, [arrays], core_ids=[0])
    return r.results[0]["out_0"]
```

```python
from contextlib import ExitStack

import concourse.bass as bass
from concourse import mybir

F32 = mybir.dt.float32
BF16 = mybir.dt.bfloat16
I32 = mybir.dt.int32
ALU = mybir.AluOpType
ACT = mybir.ActivationFunctionType
AX = mybir.AxisListType

P = 128
N = 6250
E = 106250
D = 128
NB = -(-N // P)
GB = 5
NBP = -(-NB // (2 * GB)) * 2 * GB
NP = NBP * P
W = 2
TE = W * P
T = -(-E // TE)
TP = T + 1
U = 8
G = 2
NG = U // G
GW = G * W
K = -(-(T + NB - 1) // U) * U
KJ = -(-K // P)
KP = KJ * P
KW = KP * W
ITER = K // U
C = D + 4
DEN, MAX, ER = D, D + 1, D + 2
R = D + 1
CH = 400
NCH = NP // CH
BIG = -1.0e30
EPS = 1e-5
GIN = 5
TABLES = 4
L1U = 8
L1T = -(-E // P)
L1I = -(-L1T // (2 * L1U))
PAD_DST = NBP * P
L2VECS = ("b", "g", "be")
GVECS = ("b1", "b2", "bn1_g", "bn1_b", "bn2_g", "bn2_b", "bn3_g", "bn3_b")


def build(nc, a, out):
    ctx = ExitStack()
    with ctx:
        pe, dve, act, pool, sp = nc.tensor, nc.vector, nc.scalar, nc.gpsimd, nc.sync

        def sb(name, cols, dt=F32, parts=P):
            return ctx.enter_context(nc.sbuf_tensor(name, [parts, cols], dt))

        def dram(name, shape, dt=F32):
            return nc.dram_tensor(name, shape, dt).ap()

        src_pad = dram("src_pad", (TP, TE), I32)
        dst_pad = dram("dst_pad", (TP, TE), I32)
        ea3_pad = dram("ea3_pad", (TP, TE * 3))
        idx_steps = dram("idx_steps", (K // G, P, GW), I32)
        dloc_rows = dram("dloc_rows", (KP, TE), BF16)
        tail_rows = dram("tail_rows", (L1U * P, D))
        gat_rows = dram("gat_rows", (NP, R))
        gin_rows = dram("gin_rows", (NP, D))
        sums = [dram(f"edge_sums{t}", (NP, D)) for t in range(TABLES)]

        X = sb("x_nodes", NBP * D)
        S = sb("state", NBP * C)
        XTa = sb("xT_a", NP)
        XTb = sb("xT_b", NP)
        dloc_cols = sb("dloc_cols", KW)
        al_cols = sb("al_cols", 4 * KW)
        btab = sb("block_of_step", U + KP, I32, 1)
        ident = sb("ident", P)
        ones = sb("ones", P)
        lower = sb("lower", P)
        iota_p = sb("iota_p", 1)
        dump = sb("dump", 1)
        iota_row = sb("iota_row", P)
        Wst = sb("w_static", 8 * D)
        Wext = sb("w_ext", 4 * (D + 2))
        vec = sb("vectors", 128)
        aff = sb("affine", 2)
        stat = sb("stats", 6 * 16)
        small = sb("small", 64)
        aloop = sb("aloop", 3)
        rows5 = [sb(f"rows5_{h}", GB * D) for h in range(2)]
        gst = [sb(f"gat_stage{h}", GB * R) for h in range(2)]
        idx = [sb(f"idx{g}", GW, I32) for g in range(NG)]
        grow = [sb(f"grow{g}", GW * R) for g in range(NG)]
        dl = [sb(f"dl{g}", GW * P, BF16) for g in range(NG)]
        mask = [sb(f"mask{g}", GW * P, BF16) for g in range(NG)]
        s_col = [sb(f"s_col{g}", GW) for g in range(NG)]
        sm = [sb(f"sm{i}", TE + 2) for i in range(4)]
        um = [sb(f"um{i}", TE + 2) for i in range(4)]
        neg = [sb(f"neg{i}", 1) for i in range(4)]
        pt = [sb(f"pt{i}", TE + 2) for i in range(8)]
        colst = [sb(f"col_stage{h}", L1U) for h in range(2)]
        pw = [sb(f"pw{i}", TE) for i in range(4)]
        PS = ctx.enter_context(nc.psum_tensor("ps", [P, 8 * 512], F32))

        def bank(i, cols=512, n=1):
            return PS[:, i * 512:i * 512 + cols] if n == 1 else PS[:, i * 512:(i + n) * 512]

        sems = {}
        for name in ("chain", "load", "load2", "store", "stage", "mm", "evac", "out",
                     "s_ready", "bcast", "old_max", "masked", "new_max", "weights", "transposed",
                     "pw_ready", "product", "summed", "leaky", "act_a", "act_b", "m_ready",
                     "rows0", "rows1", "rows2", "rows3", "idx0", "idx1", "idx2", "idx3",
                     "dl0", "dl1", "dl2", "dl3", "tab0", "tab1", "tab2", "tab3",
                     "eq", "first", "index", "open", "ld0", "ld1", "st0", "st1", "base", "memset"):
            sems[name] = ctx.enter_context(nc.semaphore(name))
        sem_list = list(sems.values())
        q = sems
        sem_range = range(min(s.num for s in sem_list), max(s.num for s in sem_list) + 1)
        assert len(sem_range) == len(sem_list)

        def end_phase(pool_dmas=()):
            for name, count in pool_dmas:
                pool.wait_ge(q[name], count)
            if pool_dmas:
                pool.dma_reset(sem_range)
            nc.all_engine_barrier(sems_to_clear=sem_range)

        def settled(eng):
            eng.sem_inc(q["open"], 1)

        class Serial:

            def __init__(self):
                self.counts = {"chain": 0, "load2": 0}
                self.last = None

            def wait(self, eng):
                if self.last:
                    eng.wait_ge(q[self.last], self.counts[self.last])

            def __call__(self, eng, ins, inc=1):
                name = "load2" if eng is pool and inc == 16 else "chain"
                self.wait(eng)
                ins().then_inc(q[name], inc)
                self.counts[name] += inc
                self.last = name

        def xb(t, c=D):
            return t[:, :].rearrange("p (b c) -> p b c", c=c)

        Xb, Sb = xb(X), xb(S, C)
        row = lambda v: v.rearrange("(a n) -> a n", a=1)
        col = lambda v: v.rearrange("(n a) -> n a", a=1)

        VB = {}

        def vcol(name):
            if name not in VB:
                VB[name] = len(VB)
            return vec[:, VB[name]:VB[name] + 1]

        s = Serial()
        s(pool, lambda: pool.memset(ones[:, :], 1.0))
        s(pool, lambda: pool.memset(ident[:, :], 0.0))
        s(pool, lambda: pool.affine_select(out=ident[:, :], in_=ident[:, :], compare_op=ALU.not_equal,
                                           fill=1.0, base=0, pattern=[[-1, P]], channel_multiplier=1))
        s(pool, lambda: pool.affine_select(out=lower[:, :], in_=ones[:, :], compare_op=ALU.is_gt,
                                           fill=0.0, base=0, pattern=[[-1, P]], channel_multiplier=1))
        s(pool, lambda: pool.iota(iota_p[:, :], pattern=[[0, 1]], base=0, channel_multiplier=1,
                                  allow_small_or_imprecise_dtypes=True))
        s(pool, lambda: pool.iota(dump[:, :], pattern=[[0, 1]], base=N, channel_multiplier=1,
                                  allow_small_or_imprecise_dtypes=True))
        s(pool, lambda: pool.iota(iota_row[:, :], pattern=[[1, P]], base=0, channel_multiplier=0,
                                  allow_small_or_imprecise_dtypes=True))
        s(dve, lambda: dve.memset(XTa[:, :], 0.0))
        s(dve, lambda: dve.memset(X[:, (NB - 1) * D:], 0.0))
        s(dve, lambda: dve.memset(vec[:, :], 0.0))
        s(dve, lambda: dve.memset(small[:, :], 0.0))
        pad_i = XTb[0:1, 0:TE * TP - E].bitcast(I32)
        zero_i = XTb[0:1, 2048:2048 + TE * TP - E].bitcast(I32)
        s(dve, lambda: dve.memset(zero_i, 0))
        s(dve, lambda: dve.memset(pad_i, PAD_DST))
        flat = lambda t: t.rearrange("t e -> (t e)")
        zeros = XTa[:, 0:D]
        loads = []

        def load(dst, src):
            loads.append((dst, src))

        full = N // P
        load(Xb[:, 0:full, :], a["x"][0:full * P, :].rearrange("(b p) f -> p b f", p=P))
        load(Xb[0:N - full * P, full, :], a["x"][full * P:N, :])
        for pad, name, fill in ((src_pad, "src", zero_i), (dst_pad, "dst", pad_i)):
            load(flat(pad)[0:E].rearrange("(p c) -> p c", p=125), a[name].rearrange("(p c) -> p c", p=125))
            load(row(flat(pad)[E:]), fill)
        load(flat(ea3_pad)[0:3 * E].rearrange("(p c) -> p c", p=125),
             a["edge_attr_3"].rearrange("(p c) k -> p (c k)", p=125))
        n_pad = 3 * (TE * TP - E)
        load(row(flat(ea3_pad)[3 * E:]), XTa[0:1, 0:n_pad])
        tail0 = (2 * L1I - 1) * L1U * P
        load(tail_rows[0:E - tail0, :], a["edge_attr_128"][tail0:E, :])
        left = L1U * P - (E - tail0)
        for r in range(0, left, P):
            n = min(P, left - r)
            load(tail_rows[E - tail0 + r:E - tail0 + r + n, :], XTa[0:n, 0:D])
        for t in range(TABLES):
            load(sums[t].rearrange("(b p) f -> p b f", p=P), XTa[:, :].rearrange("p (b f) -> p b f", f=D))
        gat_w = [a["L0_gnn_W"]] + [a[f"L2_gnn_W{l}"] for l in (1, 2, 3)]
        for l in range(4):
            load(Wext[:, l * (D + 2):l * (D + 2) + D], gat_w[l])
        l1w = [a["L1_gnn_W_c"][0:D, :], a["L1_gnn_W_c"][D:2 * D, :], a["L1_gnn_W_c"][2 * D:3 * D, :],
               a["L1_gnn_W1"], a["L1_gnn_W2"], a["L1_gnn_W3"]]
        for i, w in enumerate(l1w):
            load(Wst[:, i * D:(i + 1) * D], w)
        load(vcol("gf"), a["L1_gnn_global_feat"].rearrange("a n -> n a"))
        for v in ("b_c", "b1", "b2", "b3"):
            load(vcol("L1" + v), col(a["L1_gnn_" + v]))
        for l in range(3):
            for v in L2VECS:
                load(vcol(f"L2{v}{l}"), col(a[f"L2_gnn_{v}{l + 1}"]))
        for l in range(GIN):
            for v in GVECS:
                load(vcol(f"G{v}{l}"), col(a["L3_gnn_" + v][l, :]))
        for l, (n1, n2) in enumerate([("L0_gnn_attn_l", "L0_gnn_attn_r")] +
                                     [(f"L2_gnn_as{l}", f"L2_gnn_ad{l}") for l in (1, 2, 3)]):
            load(vcol(f"as{l}"), col(a[n1]))
            load(vcol(f"ad{l}"), col(a[n2]))
        for l in range(3):
            load(vcol(f"ae{l}"), col(a[f"L2_gnn_ae{l + 1}"]))
            for c in range(3):
                load(vcol(f"We{l}{c}"), col(a[f"L2_gnn_We{l + 1}"][c, :]))
        for eng in (sp, act):
            s.wait(eng)
        with nc.allow_non_contiguous_dma(reason="vectors laid along partitions"):
            for i, (dst, src) in enumerate(loads):
                (sp, act)[i % 2].dma_start(dst, src).then_inc(q["load"], 16)
            firsts = XTb[0:1, 1024:1024 + T].bitcast(I32)
            sp.dma_start(firsts, row(a["dst"][0:1 + (T - 1) * TE:TE])).then_inc(q["load"], 16)
        for eng in (pe, dve, act, pool, sp):
            eng.wait_ge(q["load"], 16 * (len(loads) + 1))
        end_phase()

        start_row = XTb[0:1, 2048:2048 + TP]
        cmp_out = XTb[:, 4096:4096 + TP]
        kcol = small[:, 0:KJ]
        tcol = small[:, 8:8 + KJ]
        bcol = small[:, 16:16 + KJ]
        b128 = small[:, 24:24 + KJ]
        tcol_i = idx[0][:, 0:1]
        srcR = S[:, 0:KW].bitcast(I32)
        dstR = S[:, KW:2 * KW].bitcast(I32)
        eaR = S[:, 2 * KW:5 * KW]
        dlocR = XTa[:, 0:KW]
        srcF = XTa[:, KW:2 * KW]
        alR = XTa[:, 2 * KW:3 * KW]
        dlocB = XTa[:, 3 * KW:4 * KW].bitcast(BF16)[:, 0:KW]
        srcI = XTa[:, 4 * KW:5 * KW].bitcast(I32)
        s = Serial()
        s(pool, lambda: pool.iota(kcol, pattern=[[P, KJ]], base=0, channel_multiplier=1,
                                  allow_small_or_imprecise_dtypes=True))
        s(pool, lambda: pool.iota(start_row, pattern=[[1, TP]], base=0, channel_multiplier=0,
                                  allow_small_or_imprecise_dtypes=True))
        s(dve, lambda: dve.tensor_scalar(firsts, firsts, 7, None, ALU.logical_shift_right))
        s(dve, lambda: dve.memset(firsts[:, 0:1], 0))
        s(dve, lambda: dve.tensor_copy(XTb[0:1, 3072:3072 + T], firsts))
        s(dve, lambda: dve.tensor_tensor(start_row[:, 0:T], start_row[:, 0:T], XTb[0:1, 3072:3072 + T], ALU.add))
        s(dve, lambda: dve.memset(start_row[:, T:TP], float(T + NB - 1)))
        for o in range(0, TP, 512):
            n = min(512, TP - o)
            s(pe, lambda: pe.matmul(PS[:, o:o + n], ones[0:1, :], start_row[:, o:o + n], start=True, stop=True))
        for j in range(KJ):
            s(dve, lambda: dve.tensor_scalar(cmp_out, PS[:, 0:TP], kcol[:, j:j + 1], 0.0, ALU.is_le, ALU.add,
                                             accum_out=tcol[:, j:j + 1]))
        s(dve, lambda: dve.tensor_scalar(tcol, tcol, 1.0, None, ALU.subtract))
        s(dve, lambda: dve.tensor_tensor(bcol, kcol, tcol, ALU.subtract))
        s(dve, lambda: dve.tensor_scalar(b128, bcol, float(P), None, ALU.mult))
        for j in range(KJ):
            s(dve, lambda: dve.tensor_copy(tcol_i, tcol[:, j:j + 1]))
            for dst, tab, w in ((srcR, src_pad, TE), (dstR, dst_pad, TE), (eaR, ea3_pad, 3 * TE)):
                s(pool, lambda: pool.indirect_dma_start(dst[:, j * w:(j + 1) * w], None, tab[:, :],
                                                        bass.IndirectOffsetOnAxis(tcol_i, 0)), 16)
        s(dve, lambda: dve.tensor_copy(srcF, srcR))
        s(dve, lambda: dve.tensor_copy(dlocR, dstR))
        for j in range(KJ):
            v = dlocR[:, j * TE:(j + 1) * TE]
            s(dve, lambda: dve.tensor_scalar(v, v, b128[:, j:j + 1], None, ALU.subtract))
        s(dve, lambda: dve.tensor_copy(dlocB, dlocR))
        s(sp, lambda: sp.dma_start(dloc_rows.rearrange("(j p) e -> p j e", p=P),
                                   dlocB.rearrange("p (j e) -> p j e", e=TE)), 16)

        def to_cols(src, dst):
            for i in range(KJ * W):
                s(pe, lambda: pe.transpose(PS[:, 2048 + i * P:2048 + (i + 1) * P], src[:, i * P:(i + 1) * P],
                                           ident[:, :]))
            s(dve, lambda: dve.tensor_copy(dst.rearrange("p (j k w) -> p j w k", j=KJ, w=W),
                                           PS[:, 2048:2048 + KW].rearrange("p (j w k) -> p j w k", j=KJ, w=W)))

        to_cols(srcF, srcI)
        with nc.allow_non_contiguous_dma(reason="four sources a partition"):
            s(sp, lambda: sp.dma_start(idx_steps.rearrange("g p c -> p g c"),
                                       srcI[:, 0:K * W].rearrange("p (g c) -> p g c", c=GW)), 16)
        to_cols(dlocR, dloc_cols[:, :])
        s(pe, lambda: pe.transpose(PS[0:KJ, 0:P], bcol, ident[:, :]))
        s(dve, lambda: dve.tensor_copy(rows5[0][0:KJ, 0:P].bitcast(I32), PS[0:KJ, 0:P]))
        s(dve, lambda: dve.memset(btab[:, 0:U], 0))
        s(sp, lambda: sp.dma_start(btab[0:1, U:U + KP].rearrange("a (j p) -> a j p", p=P),
                                   rows5[0][0:KJ, 0:P].bitcast(I32)), 16)
        vl = small[:, 32:41]
        eam = small[:, 41:44]
        tmp3 = small[:, 48:51]
        for l in range(3):
            w0 = VB[f"We{l}0"]
            s(pe, lambda: pe.matmul(PS[:, 3 * l:3 * l + 3], vcol(f"ae{l}").to_broadcast([P, P]),
                                    vec[:, w0:w0 + 3], start=True, stop=True))
        s(dve, lambda: dve.tensor_copy(vl, PS[:, 0:9]))
        ea_all = S[0:125, 0:2550]
        for l in range(3):
            for c in range(3):
                v = eaR.rearrange("p (n c) -> p n c", c=3)[:, :, c]
                w = vl[:, 3 * l + c:3 * l + c + 1]
                if c == 0:
                    s(dve, lambda: dve.tensor_scalar(alR, v, w, None, ALU.mult))
                else:
                    s(dve, lambda: dve.scalar_tensor_tensor(alR, v, w, alR, ALU.mult, ALU.add))
            to_cols(alR, al_cols[:, (l + 1) * KW:(l + 2) * KW])
        s(dve, lambda: dve.memset(al_cols[:, 0:KW], 0.0))
        s(sp, lambda: sp.dma_start(ea_all, a["edge_attr_3"].rearrange("(p c) k -> p (c k)", p=125)), 16)
        s(dve, lambda: dve.tensor_reduce(tmp3[0:125, :], ea_all.rearrange("p (n c) -> p c n", c=3), AX.X, ALU.add))
        s(pe, lambda: pe.matmul(PS[:, 0:3], ones[0:125, :], tmp3[0:125, :], start=True, stop=True))
        s(dve, lambda: dve.tensor_scalar(eam, PS[:, 0:3], 1.0 / E, None, ALU.mult))
        for l in range(3):
            s(dve, lambda: dve.tensor_tensor(tmp3, eam, vl[:, 3 * l:3 * l + 3], ALU.mult))
            s(dve, lambda: dve.tensor_reduce(aloop[:, l:l + 1], tmp3, AX.X, ALU.add))
        for l in range(4):
            o = l * (D + 2)
            v0 = VB[f"as{l}"]
            s(pe, lambda: pe.transpose(PS[:, 0:D], Wext[:, o:o + D], ident[:, :]))
            s(dve, lambda: dve.tensor_copy(rows5[0][:, 0:D], PS[:, 0:D]))
            s(pe, lambda: pe.matmul(PS[:, 0:2], rows5[0][:, 0:D], vec[:, v0:v0 + 2], start=True, stop=True))
            s(dve, lambda: dve.tensor_copy(Wext[:, o + D:o + D + 2], PS[:, 0:2]))
        c1 = vcol("c1")
        s(pe, lambda: pe.matmul(PS[:, 0:1], Wst[:, 2 * D:3 * D], vcol("gf"), start=True, stop=True))
        s(dve, lambda: dve.tensor_tensor(c1, PS[:, 0:1], vcol("L1b_c"), ALU.add))
        end_phase([("load2", s.counts["load2"])])

        def group_src(t, c):
            def at(g):
                return t[:, bass.ds(g * (GB * c), GB * c)].rearrange("p (b c) -> p b c", c=c)[:, :, 0:D]
            return at

        HALF = NBP // (2 * GB)

        def turn():
            with pe.Fori(0, HALF) as it:
                for h in range(2):
                    pe.wait_ge(q["stage"], it * 2 + h + 1)
                    pe.wait_ge(q["evac"], it * 2 + h + 1)
                    for u in range(GB):
                        pe.transpose(PS[:, h * 1024 + u * D:h * 1024 + (u + 1) * D],
                                     rows5[h][:, u * D:(u + 1) * D], ident[:, :]).then_inc(q["mm"], 1)

        def node_to_feature(t, c, dst):
            src = group_src(t, c)
            pe.sem_inc(q["mm"], 2 * GB)
            dve.sem_inc(q["evac"], 2)
            with act.Fori(0, HALF) as it:
                for h in range(2):
                    act.wait_ge(q["mm"], it * (2 * GB) + (h + 1) * GB)
                    act.activation(rows5[h][:, :].rearrange("p (b c) -> p b c", c=D), src(it * 2 + h),
                                   ACT.Copy).then_inc(q["stage"], 1)
            turn()
            with dve.Fori(0, HALF) as it:
                for h in range(2):
                    dve.wait_ge(q["mm"], it * (2 * GB) + (h + 3) * GB)
                    dve.tensor_copy(dst[:, bass.ds((it * 2 + h) * (GB * P), GB * P)],
                                    PS[:, h * 1024:h * 1024 + GB * P]).then_inc(q["evac"], 1)
            end_phase()

        def feature_to_node(src, t, c, func, scale, shift, rows=None):
            pe.sem_inc(q["mm"], 2 * GB)
            dve.sem_inc(q["evac"], 2)
            with act.Fori(0, HALF) as it:
                for h in range(2):
                    act.wait_ge(q["mm"], it * (2 * GB) + (h + 1) * GB)
                    act.activation(rows5[h][:, :], src[:, bass.ds((it * 2 + h) * (GB * P), GB * P)],
                                   func, bias=shift, scale=scale).then_inc(q["stage"], 1)
            turn()
            with dve.Fori(0, HALF) as it:
                for h in range(2):
                    dve.wait_ge(q["mm"], it * (2 * GB) + (h + 3) * GB)
                    dve.tensor_copy(group_src(t, c)(it * 2 + h),
                                    PS[:, h * 1024:h * 1024 + GB * P].rearrange("p (b c) -> p b c", c=D)
                                    ).then_inc(q["evac"], 1)
            if rows is not None:
                store_rows(t, c, rows)
            end_phase()

        def store_rows(t, c, rows):
            sp.wait_ge(q["evac"], 2 + 2 * HALF)
            sp.dma_start(rows.rearrange("(b p) f -> p b f", p=P), xb(t, c)[:, :, 0:D]).then_inc(q["out"], 16)
            sp.wait_ge(q["out"], 16)

        def linear(src, w, dst, bias, func=None, scale=None, shift=None, second=None):
            if func is not None:
                with act.Fori(0, NCH // 2) as it:
                    for h in range(2):
                        act.wait_ge(q["mm"], it * 2 + h + 1)
                        act.activation(rows5[h][:, 0:CH], src[:, bass.ds((it * 2 + h) * CH, CH)], func,
                                       bias=shift, scale=scale).then_inc(q["stage"], 1)
            pe.sem_inc(q["mm"], 2)
            dve.sem_inc(q["evac"], 2)
            with pe.Fori(0, NCH // 2) as it:
                for h in range(2):
                    pe.wait_ge(q["evac"], it * 2 + h + 1)
                    if func is not None:
                        pe.wait_ge(q["stage"], it * 2 + h + 1)
                        v = rows5[h][:, 0:CH]
                    else:
                        v = src[:, bass.ds((it * 2 + h) * CH, CH)]
                    m = pe.matmul(bank(h, CH), w, v, start=True, stop=second is None)
                    if second is not None:
                        m = pe.matmul(bank(h, CH), second[1], second[0][:, bass.ds((it * 2 + h) * CH, CH)],
                                      start=False, stop=True)
                    m.then_inc(q["mm"], 1)
            with dve.Fori(0, NCH // 2) as it:
                for h in range(2):
                    dve.wait_ge(q["mm"], it * 2 + h + 3)
                    dve.tensor_scalar(dst[:, bass.ds((it * 2 + h) * CH, CH)], bank(h, CH), bias, None,
                                      ALU.add).then_inc(q["evac"], 1)
            end_phase()

        def norm_stats(src, gamma, beta, relu=False):
            s = Serial()
            if relu:
                s(act, lambda: act.activation(src[:, :], src[:, :], ACT.Relu, bias=aff[:, 1:2], scale=aff[:, 0:1]))
            n = -(-N // 512)
            for i in range(n):
                s(dve, lambda: dve.bn_stats(stat[:, 6 * i:6 * i + 6], src[:, 512 * i:min(512 * i + 512, N)]))
            s(dve, lambda: dve.bn_aggr(small[:, 0:2], stat[:, 0:6 * n]))
            s(dve, lambda: dve.tensor_scalar(small[:, 2:3], small[:, 1:2], EPS, None, ALU.add))
            s(act, lambda: act.activation(small[:, 3:4], small[:, 2:3], ACT.Sqrt))
            s(dve, lambda: dve.reciprocal(small[:, 4:5], small[:, 3:4]))
            s(dve, lambda: dve.tensor_tensor(aff[:, 0:1], small[:, 4:5], gamma, ALU.mult))
            s(dve, lambda: dve.tensor_tensor(small[:, 5:6], small[:, 0:1], aff[:, 0:1], ALU.mult))
            s(dve, lambda: dve.tensor_tensor(aff[:, 1:2], beta, small[:, 5:6], ALU.subtract))
            end_phase()

        def layer_norm():
            s = Serial()
            mean = XTa[:, 0:NBP]
            var = XTa[:, NBP:2 * NBP]
            sq = XTb[:, :]
            bc = lambda t: t.rearrange("p (b a) -> p b a", a=1).to_broadcast([P, NBP, D])
            s(dve, lambda: dve.tensor_tensor(Xb, Xb, Sb[:, :, 0:D], ALU.add))
            s(dve, lambda: dve.tensor_reduce(mean, Xb, AX.X, ALU.add))
            s(dve, lambda: dve.tensor_scalar(mean, mean, 1.0 / D, None, ALU.mult))
            s(dve, lambda: dve.tensor_tensor(Xb, Xb, bc(mean), ALU.subtract))
            s(act, lambda: act.activation(sq, X[:, :], ACT.Square))
            s(dve, lambda: dve.tensor_reduce(var, xb(XTb), AX.X, ALU.add))
            s(dve, lambda: dve.tensor_scalar(var, var, 1.0 / D, EPS, ALU.mult, ALU.add))
            s(act, lambda: act.activation(mean, var, ACT.Sqrt))
            s(dve, lambda: dve.reciprocal(var, mean))
            s(dve, lambda: dve.tensor_tensor(Xb, Xb, bc(var), ALU.mult))
            end_phase()

        def project(l, keep):
            if not keep:
                dve.memset(S[:, :], 0.0).then_inc(q["memset"], 1)
                dve.wait_ge(q["memset"], 1)
                dve.memset(Sb[:, :, MAX], BIG).then_inc(q["memset"], 1)
            else:
                dve.memset(Sb[:, :, DEN], 1.0).then_inc(q["memset"], 1)
            W2 = D + 2
            pe.sem_inc(q["mm"], 2)
            dve.sem_inc(q["evac"], 2)
            act.sem_inc(q["out"], 4)
            for h in range(2):
                sp.sem_inc(q[f"st{h}"], 16)
            with act.Fori(0, HALF) as it:
                for h in range(2):
                    act.wait_ge(q["mm"], it * 2 + h + 1)
                    act.activation(rows5[h][:, :], XTa[:, bass.ds((it * 2 + h) * (GB * P), GB * P)],
                                   ACT.Identity, bias=aff[:, 1:2], scale=aff[:, 0:1]).then_inc(q["stage"], 1)
                    act.wait_ge(q["mm"], it * 2 + h + 3)
                    act.wait_ge(q[f"st{h}"], it * 16 + 16)
                    for b0, n in ((0, 3), (3, GB - 3)):
                        v = PS[:, h * 1024 + b0 // 3 * 512:h * 1024 + b0 // 3 * 512 + n * W2]
                        act.activation(gst[h][:, b0 * R:(b0 + n) * R].rearrange("p (b c) -> p b c", c=R),
                                       v.rearrange("p (b c) -> p b c", c=W2)[:, :, 0:R], ACT.Copy
                                       ).then_inc(q["out"], 1)
            with pe.Fori(0, HALF) as it:
                for h in range(2):
                    pe.wait_ge(q["stage"], it * 2 + h + 1)
                    pe.wait_ge(q["evac"], it * 2 + h + 1)
                    for u in range(GB):
                        o = h * 1024 + u // 3 * 512 + u % 3 * W2
                        m = pe.matmul(PS[:, o:o + W2], rows5[h][:, u * P:(u + 1) * P],
                                      Wcur[:, :], start=True, stop=True)
                    m.then_inc(q["mm"], 1)
            dve.wait_ge(q["memset"], 1 if keep else 2)
            with dve.Fori(0, HALF) as it:
                for h in range(2):
                    dve.wait_ge(q["out"], (it * 2 + h) * 2 + 6)
                    for b0, n in ((0, 3), (3, GB - 3)):
                        o = h * 1024 + b0 // 3 * 512
                        v = PS[:, o:o + n * W2].rearrange("p (b c) -> p b c", c=W2)
                        st = S[:, bass.ds((it * 2 + h) * (GB * C) + b0 * C, n * C)] \
                            .rearrange("p (b c) -> p b c", c=C)
                        if keep:
                            dve.tensor_copy(st[:, :, 0:D], v[:, :, 0:D])
                            dve.tensor_scalar(st[:, :, MAX:MAX + 1], v[:, :, D:D + 1], cur[:, 3:4], None, ALU.add)
                        last = dve.tensor_copy(st[:, :, ER:ER + 1], v[:, :, D + 1:D + 2])
                    last.then_inc(q["evac"], 1)
            with sp.Fori(0, HALF) as it:
                for h in range(2):
                    sp.wait_ge(q["out"], (it * 2 + h) * 2 + 6)
                    sp.dma_start(gat_rows[bass.ds((it * 2 + h) * (GB * P), GB * P), :]
                                 .rearrange("(b p) f -> p b f", p=P),
                                 gst[h][:, :].rearrange("p (b c) -> p b c", c=R)).then_inc(q[f"st{h}"], 16)
            for h in range(2):
                sp.wait_ge(q[f"st{h}"], 16 * HALF + 16)
            end_phase()

        block_regs = {e.engine: [e.alloc_register(f"block{i}") for i in range(U + 5)] for e in (dve, act)}
        Wcur = sb("w_cur", D + 2)
        cur = sb("cur", 4)
        def fetch(table, width):
            def sp_part(it, first):
                for g in range(NG):
                    if not first:
                        sp.wait_ge(q[f"rows{g}"], it * (16 * GW))
                    sp.dma_start(idx[g][:, :], idx_steps[bass.ds(it * NG + g, 1), :, :]
                                 .rearrange("a p c -> (a p) c")).then_inc(q[f"idx{g}"], 16)
                    if width == R:
                        sp.wait_ge(q["m_ready"], it * NG + g + 1)
                        sp.dma_start(dl[g][:, :], dloc_rows[bass.ds(it * U + g * G, G), :]
                                     .rearrange("(a s) e -> a (s e)", a=1).to_broadcast([P, GW * P])
                                     ).then_inc(q[f"dl{g}"], 16)

            sp_part(0, True)
            with sp.Fori(1, ITER) as it:
                sp_part(it, False)
            if width == R:
                dve.sem_inc(q["m_ready"], NG)
            pe.sem_inc(q["product"], U)
            with pool.Fori(0, ITER) as it:
                for g in range(NG):
                    pool.wait_ge(q[f"idx{g}"], it * 16 + 16)
                    pool.wait_ge(q["product"], it * U + (g + 1) * G)
                    settled(pool)
                    for u in range(GW):
                        pool.indirect_dma_start(grow[g][:, u * R:u * R + width], None, table[:, :],
                                                bass.IndirectOffsetOnAxis(idx[g][:, u:u + 1], 0)
                                                ).then_inc(q[f"rows{g}"], 16)

        BS, BP, BO = 0, 2, 4

        def pipeline(eng, body, lag, first, last):
            def part(base, gbase, us, begin, end):
                blocks = {}
                lo = 0 if begin else first
                hi = 0 if end else U + last
                if first is not None and hi > lo:
                    regs = [block_regs[eng.engine][i] for i in range(hi - lo)]
                    eng.load(regs, btab[0:1, bass.ds(base + (U + lo), hi - lo)])
                    blocks = {lo + i: eng.snap(r, min_val=0, max_val=NB - 1) for i, r in enumerate(regs)}
                for u in us:
                    body(base + u, gbase, u, lambda d, u=u: (u >= d if begin else d > u if end else True),
                         blocks)
            part(0, 0, range(U), True, False)
            with eng.Fori(1, ITER) as it:
                part(it * U, it * NG, range(U), False, False)
            part(K, ITER * NG, range(lag), False, True)

        def gat_edges(al0):
            fetch(gat_rows, R)

            def pe_body(n, gbase, u, have, blocks):
                if have(0):
                    g = u // G
                    if u % G == 0:
                        pe.wait_ge(q["s_ready"], gbase + g + 1)
                    if have(2):
                        pe.wait_ge(q["masked"], n - 1)
                    for w in range(W):
                        i = u % G * W + w
                        m = pe.matmul(bank(BS + u % 2)[:, w * P:(w + 1) * P],
                                      s_col[g][:, i:i + 1].to_broadcast([P, P]), ident[:, :],
                                      start=True, stop=True)
                    m.then_inc(q["bcast"], 1)
                if have(2):
                    v = (u - 2) % U
                    pe.wait_ge(q["weights"], n - 1)
                    for w in range(W):
                        m = pe.transpose(bank(BP + v % 2)[:, w * P:(w + 1) * P], pt[v][:, w * P:(w + 1) * P],
                                         ident[:, :])
                    m.then_inc(q["transposed"], 1)
                if have(3):
                    v = (u - 3) % U
                    pe.wait_ge(q["pw_ready"], n - 2)
                    if have(5):
                        pe.wait_ge(q["summed"], n - 4)
                    for w in range(W):
                        i = v % G * W + w
                        m = pe.matmul(bank(BO + v % 2, R), pw[v % 4][:, w * P:(w + 1) * P],
                                      grow[v // G][:, i * R:(i + 1) * R], start=w == 0, stop=w == W - 1)
                    m.then_inc(q["product"], 1)

            def load_max(n, u, blocks):
                dve.tensor_scalar(sm[u % 4][:, TE + 1:TE + 2], S[:, bass.ds(blocks[u] * C + MAX, 1)], 1.0, None,
                                  ALU.mult).then_inc(q["old_max"], 1)

            def dve_body(n, gbase, u, have, blocks):
                if have(0):
                    g = u // G
                    m = sm[u % 4]
                    if u % G == 0:
                        rows = grow[g][:, :].rearrange("p (s c) -> p s c", c=R)[:, :, D]
                        dve.wait_ge(q[f"rows{g}"], gbase * (16 * GW // NG) + 16 * GW)
                        if have(U):
                            dve.wait_ge(q["bcast"], n - (U - G))
                        dve.tensor_tensor(s_col[g][:, :], rows, al_cols[:, bass.ds(n * W + al0, GW)],
                                          ALU.add).then_inc(q["s_ready"], 1)
                        dve.wait_ge(q[f"dl{g}"], gbase * (16 // NG) + 16)
                        dve.tensor_scalar(mask[g][:, :], dl[g][:, :], iota_p[:, :], BIG, ALU.not_equal,
                                          ALU.mult).then_inc(q["m_ready"], 1)
                        dve.wait_ge(q["s_ready"], gbase + g + 1)
                        dve.memset(rows, 1.0)
                        dve.wait_ge(q["m_ready"], gbase + g + 1 + NG)
                        if u == 0 and not have(1):
                            load_max(n, u, blocks)
                    dve.wait_ge(q["bcast"], n + 1)
                    dve.wait_ge(q["old_max"], n + 1)
                    settled(dve)
                    dve.tensor_tensor_reduce(out=m[:, 0:TE], in0=bank(BS + u % 2, TE),
                                             in1=mask[g][:, u % G * TE:(u % G + 1) * TE], scale=1.0,
                                             scalar=m[:, TE + 1:TE + 2], op0=ALU.add, op1=ALU.max,
                                             accum_out=m[:, TE:TE + 1]).then_inc(q["masked"], 1)
                w = um[(u - 1) % 4]
                if have(1):
                    dve.wait_ge(q["act_a"], n)
                    dve.scalar_tensor_tensor(w[:, :], w[:, :], 0.2, w[:, :], ALU.mult, ALU.max
                                             ).then_inc(q["leaky"], 1)
                if have(0):
                    dve.wait_ge(q["masked"], n + 1)
                    dve.tensor_scalar(S[:, bass.ds(blocks[u] * C + MAX, 1)], m[:, TE:TE + 1], 1.0, None, ALU.mult
                                      ).then_inc(q["new_max"], 1)
                if have(4):
                    v = (u - 4) % U
                    st = S[:, bass.ds(blocks[u - 4] * C, R)]
                    dve.wait_ge(q["product"], n - 3 + U)
                    if have(5):
                        dve.wait_ge(q["summed"], n - 4)
                    dve.scalar_tensor_tensor(st, st, pt[v][:, TE + 1:TE + 2], bank(BO + v % 2, R),
                                             ALU.mult, ALU.add).then_inc(q["summed"], 1)
                if have(1):
                    dve.wait_ge(q["leaky"], n)
                    dve.tensor_scalar(neg[(u - 1) % 4][:, :], w[:, TE:TE + 1], -1.0, None, ALU.mult
                                      ).then_inc(q["act_b"], 1)
                if have(0):
                    dve.wait_ge(q["new_max"], n + 1)
                    load_max(n + 1, u + 1, blocks)

            def act_body(n, gbase, u, have, blocks):
                if have(0):
                    act.wait_ge(q["masked"], n + 1)
                    act.activation(um[u % 4][:, :], sm[u % 4][:, :], ACT.Identity,
                                   bias=S[:, bass.ds(blocks[u] * C + ER, 1)]).then_inc(q["act_a"], 1)
                if have(2):
                    v = (u - 2) % U
                    act.wait_ge(q["transposed"], n - 1)
                    act.activation(pw[v % 4][:, :], bank(BP + v % 2, TE), ACT.Copy).then_inc(q["pw_ready"], 1)
                if have(1):
                    v = (u - 1) % U
                    act.wait_ge(q["act_b"], n)
                    act.activation(pt[v][:, :], um[v % 4][:, :], ACT.Exp, bias=neg[v % 4][:, :]
                                   ).then_inc(q["weights"], 1)

            pipeline(pe, pe_body, 3, None, 0)
            pipeline(dve, dve_body, 4, -4, 1)
            pipeline(act, act_body, 2, 0, 0)
            end_phase([(f"rows{g}", ITER * GW * 16) for g in range(NG)])

        def gin_edges():
            fetch(gin_rows, D)

            def pe_body(n, gbase, u, have, blocks):
                g = u // G
                if u % G == 0:
                    pe.wait_ge(q[f"rows{g}"], gbase * (16 * GW // NG) + 16 * GW)
                pe.wait_ge(q["eq"], n + 1)
                if have(4):
                    pe.wait_ge(q["summed"], n - 3)
                for w in range(W):
                    i = u % G * W + w
                    m = pe.matmul(bank(u % 4, D), pw[u % 4][:, w * P:(w + 1) * P], grow[g][:, i * R:i * R + D],
                                  start=w == 0, stop=w == W - 1)
                m.then_inc(q["product"], 1)

            def dve_body(n, gbase, u, have, blocks):
                if have(0):
                    if have(4):
                        dve.wait_ge(q["product"], n - 3 + U)
                    for w in range(W):
                        m = dve.tensor_scalar(pw[u % 4][:, w * P:(w + 1) * P], iota_row[:, :],
                                              dloc_cols[:, bass.ds(n * W + w, 1)], None, ALU.is_equal)
                    m.then_inc(q["eq"], 1)
                if have(2):
                    v = (u - 2) % U
                    st = S[:, bass.ds(blocks[u - 2] * C, D)]
                    dve.wait_ge(q["product"], n - 1 + U)
                    if have(3):
                        dve.wait_ge(q["summed"], n - 2)
                    dve.tensor_tensor(st, st, bank(v % 4, D), ALU.add).then_inc(q["summed"], 1)

            pipeline(pe, pe_body, 0, None, 0)
            pipeline(dve, dve_body, 2, -2, 0)
            end_phase([(f"rows{g}", ITER * GW * 16) for g in range(NG)])

        def edge_sums():
            src_c = XTb[:, 0:2 * L1I * L1U]
            s = Serial()
            src_tiles = src_pad.rearrange("t (w e) -> (t w) e", w=W)
            nt = 2 * L1I * L1U
            nj = -(-nt // P)
            si = XTa[:, 0:nj * P].bitcast(I32)
            sf = XTa[:, nj * P:2 * nj * P]
            s(dve, lambda: dve.memset(XTa[:, 0:2 * nj * P], 0.0))
            for j in range(nj):
                n = min(P, nt - j * P)
                s(sp, lambda: sp.dma_start(si[0:n, j * P:(j + 1) * P], src_tiles[j * P:j * P + n, :]), 16)
            s(dve, lambda: dve.tensor_copy(sf, si))
            for j in range(nj):
                s(pe, lambda: pe.transpose(PS[:, j * P:(j + 1) * P], sf[:, j * P:(j + 1) * P], ident[:, :]))
            s(dve, lambda: dve.tensor_copy(src_c, PS[:, 0:2 * L1I * L1U]))
            end_phase()
            ea = [XTa[:, i * 1024:(i + 1) * 1024] for i in range(2)]
            vals = [XTa[:, 2048 + i * P:2048 + (i + 1) * P] for i in range(2 * L1U)]
            eqs = [XTb[:, 1024 + i * P:1024 + (i + 1) * P] for i in range(4)]
            junk = XTb[:, 2048:2048 + P]
            cnt = [small[:, 8 * h:8 * h + 8] for h in range(2)]
            fl = small[:, 16:24]
            to = small[:, 24:32]
            ix = [small[:, 32 + 8 * h:40 + 8 * h].bitcast(I32) for h in range(2)]
            per = 2 * L1U
            rows_of = a["edge_attr_128"]

            def ld(it, h, src):
                sp.wait_ge(q["product"], it * per + h * L1U + L1U)
                sp.dma_start(ea[h].rearrange("p (t f) -> p t f", f=D), src).then_inc(q[f"ld{h}"], 16)

            pe.sem_inc(q["product"], per)
            tile_rows = lambda v: v.rearrange("(t p) f -> p t f", p=P)
            with sp.Fori(0, L1I - 1) as it:
                for h in range(2):
                    ld(it, h, tile_rows(rows_of[bass.ds((it * 2 + h) * (L1U * P), L1U * P), :]))
            ld(L1I - 1, 0, tile_rows(rows_of[(L1I - 1) * 2 * L1U * P:((L1I - 1) * 2 + 1) * L1U * P, :]))
            ld(L1I - 1, 1, tile_rows(tail_rows))
            act.sem_inc(q["evac"], 4)

            def pe_part(it, first):
                for u in range(per):
                    h = u // L1U
                    pe.wait_ge(q["s_ready"], it * 2 + h + 1)
                    if not (first and u < 2):
                        pe.wait_ge(q["eq"], it * per + u - 1)
                    pe.matmul(bank(u % 2, P), colst[h][:, u % L1U:u % L1U + 1].to_broadcast([P, P]), ident[:, :],
                              start=True, stop=True).then_inc(q["bcast"], 1)
                    if not (first and u < 1):
                        prod(it, u - 1, first and u - 1 < 4)

            def prod(it, u, fresh):
                h = (u % per) // L1U
                n = it * per + u
                if u % L1U == 0:
                    pe.wait_ge(q[f"ld{h}"], it * 16 + 16 if u >= 0 else it * 16)
                pe.wait_ge(q["eq"], n + 1)
                pe.wait_ge(q["evac"], n + 1)
                pe.matmul(bank(2 + u % 4, P), eqs[u % 4], ea[h][:, u % L1U * D:(u % L1U + 1) * D],
                          start=True, stop=True).then_inc(q["product"], 1)

            pe_part(0, True)
            with pe.Fori(1, L1I) as it:
                pe_part(it, False)
            prod(L1I, -1, False)

            def dve_part(it, first):
                for h in range(2):
                    c = colst[h]
                    if not first:
                        dve.wait_ge(q["bcast"], it * per - per + (h + 1) * L1U)
                    dve.tensor_copy(c[:, :], src_c[:, bass.ds((it * 2 + h) * L1U, L1U)]
                                    if not first else src_c[:, h * L1U:(h + 1) * L1U]).then_inc(q["s_ready"], 1)
                    dve.wait_ge(q["s_ready"], it * 2 + h + 1)
                    for u in range(L1U):
                        n = it * per + h * L1U + u
                        k = h * L1U + u
                        dve.wait_ge(q["bcast"], n + 1)
                        if not (first and k < 4):
                            dve.wait_ge(q["product"], n - 3 + per)
                        dve.tensor_scalar(eqs[k % 4], bank(k % 2, P), c[:, u:u + 1], None, ALU.is_equal
                                          ).then_inc(q["eq"], 1)
                        dve.wait_ge(q["eq"], n + 1)
                        settled(dve)
                        dve.tensor_tensor_reduce(out=junk, in0=eqs[k % 4], in1=lower[:, :], scale=1.0, scalar=0.0,
                                                 op0=ALU.mult, op1=ALU.add, accum_out=cnt[h][:, u:u + 1]
                                                 ).then_inc(q["first"], 1)
                    g0 = it * 2 + h
                    dve.wait_ge(q["first"], it * per + (h + 1) * L1U)
                    dve.tensor_scalar(fl, cnt[h], 0.5, None, ALU.is_gt).then_inc(q["act_a"], 1)
                    dve.tensor_scalar(to, c[:, :], dump[:, :], -1.0, ALU.subtract, ALU.mult).then_inc(q["act_a"], 1)
                    dve.wait_ge(q["act_a"], g0 * 4 + 2)
                    dve.tensor_tensor(to, to, fl, ALU.mult).then_inc(q["act_a"], 1)
                    dve.wait_ge(q["act_a"], g0 * 4 + 3)
                    dve.tensor_tensor(to, to, c[:, :], ALU.add).then_inc(q["act_a"], 1)
                    dve.wait_ge(q["act_a"], g0 * 4 + 4)
                    if not first:
                        for t in range(TABLES):
                            dve.wait_ge(q[f"tab{t}"], it * (16 * per // TABLES) - (1 - h) * (16 * L1U // TABLES))
                    dve.tensor_copy(ix[h], to).then_inc(q["index"], 1)

            dve_part(0, True)
            with dve.Fori(1, L1I) as it:
                dve_part(it, False)

            def act_part(it, first):
                for u in range(per):
                    n = it * per + u
                    act.wait_ge(q["product"], n + 1 + per)
                    if not first:
                        act.wait_ge(q[f"tab{u % TABLES}"], it * (16 * per // TABLES) - 16 * (per // TABLES - 1 - u // TABLES))
                    act.activation(vals[u], bank(2 + u % 4, P), ACT.Copy).then_inc(q["evac"], 1)

            act_part(0, True)
            with act.Fori(1, L1I) as it:
                act_part(it, False)

            def pool_part(it, first):
                for u in range(per):
                    h = u // L1U
                    t = u % TABLES
                    pool.wait_ge(q["index"], it * 2 + h + 1)
                    pool.wait_ge(q["evac"], it * per + u + 1 + 4)
                    if not (first and u < TABLES):
                        pool.wait_ge(q[f"tab{t}"], it * (16 * per // TABLES) + 16 * (u // TABLES))
                    settled(pool)
                    pool.indirect_dma_start(sums[t][:, :], bass.IndirectOffsetOnAxis(ix[h][:, u % L1U:u % L1U + 1], 0),
                                            vals[u], None, compute_op=ALU.add).then_inc(q[f"tab{t}"], 16)

            pool_part(0, True)
            with pool.Fori(1, L1I) as it:
                pool_part(it, False)
            end_phase([(f"tab{t}", L1I * per // TABLES * 16) for t in range(TABLES)])


        s = Serial()
        s(dve, lambda: dve.memset(aff[:, 0:1], 1.0))
        s(dve, lambda: dve.memset(aff[:, 1:2], 0.0))
        s(dve, lambda: dve.tensor_copy(Wcur[:, :], Wext[:, 0:D + 2]))
        end_phase()
        node_to_feature(X, D, XTa)
        project(0, False)
        gat_edges(0)

        def divide_state(floor, has):
            s = Serial()
            den = XTb[:, 0:NBP]
            flag = XTb[:, NBP:2 * NBP]
            s(dve, lambda: dve.tensor_scalar(den, Sb[:, :, DEN], floor[1], None, floor[0]))
            s(dve, lambda: dve.reciprocal(den, den))
            if has:
                s(dve, lambda: dve.tensor_scalar(flag, Sb[:, :, MAX], BIG / 2, None, ALU.is_gt))
                s(dve, lambda: dve.tensor_tensor(den, den, flag, ALU.mult))
            s(dve, lambda: dve.tensor_tensor(Sb[:, :, 0:D], Sb[:, :, 0:D],
                                             den.rearrange("p (b a) -> p b a", a=1).to_broadcast([P, NBP, D]),
                                             ALU.mult))
            end_phase()

        divide_state((ALU.max, 1e-9), True)
        layer_norm()

        edge_sums()
        s = Serial()
        tab = lambda t: sums[t].rearrange("(b p) f -> p b f", p=P)
        s(sp, lambda: sp.dma_start(Sb[:, :, 0:D], tab(0)), 16)
        s(sp, lambda: sp.dma_start(xb(XTa), tab(1)), 16)
        s(sp, lambda: sp.dma_start(xb(XTb), tab(2)), 16)
        s(dve, lambda: dve.tensor_tensor(Sb[:, :, 0:D], Sb[:, :, 0:D], xb(XTa), ALU.add))
        s(sp, lambda: sp.dma_start(xb(XTa), tab(3)), 16)
        s(dve, lambda: dve.tensor_tensor(xb(XTb), xb(XTb), xb(XTa), ALU.add))
        s(dve, lambda: dve.tensor_tensor(Sb[:, :, 0:D], Sb[:, :, 0:D], xb(XTb), ALU.add))
        end_phase()
        node_to_feature(X, D, XTa)
        node_to_feature(S, C, XTb)
        wst = lambda i: Wst[:, i * D:(i + 1) * D]

        def softplus(t):
            s = Serial()
            tmp = S[:, 0:NP]
            s(act, lambda: act.activation(tmp, t[:, :], ACT.Abs))
            s(act, lambda: act.activation(tmp, tmp, ACT.Exp, scale=-1.0))
            s(act, lambda: act.activation(tmp, tmp, ACT.Ln, bias=1.0))
            s(dve, lambda: dve.scalar_tensor_tensor(t[:, :], t[:, :], 0.0, tmp, ALU.max, ALU.add))
            end_phase()

        linear(XTa, wst(0), S, c1, second=(XTb, wst(1)))
        linear(S, wst(3), XTb, vcol("L1b1"))
        softplus(XTb)
        linear(XTb, wst(4), XTa, vcol("L1b2"))
        softplus(XTa)
        linear(XTa, wst(5), XTb, vcol("L1b3"))
        feature_to_node(XTb, S, C, ACT.Copy, 1.0, 0.0)
        layer_norm()

        node_to_feature(X, D, XTa)
        with nc.Fori(0, 3) as l:
            s = Serial()
            s(dve, lambda: dve.tensor_copy(Wcur[:, :], Wext[:, bass.ds(l * (D + 2) + (D + 2), D + 2)]))
            s(dve, lambda: dve.tensor_copy(cur[:, 0:3], vec[:, bass.ds(l * 3 + VB["L2b0"], 3)]))
            s(dve, lambda: dve.tensor_copy(cur[:, 3:4], aloop[:, bass.ds(l, 1)]))
            end_phase()
            project(l, True)
            gat_edges(l * KW + KW)
            divide_state((ALU.add, 1e-16), False)
            node_to_feature(S, C, XTa)
            s = Serial()
            s(dve, lambda: dve.tensor_scalar(XTa[:, :], XTa[:, :], cur[:, 0:1], None, ALU.add))
            s(dve, lambda: dve.scalar_tensor_tensor(XTa[:, :], XTa[:, :], 0.01, XTa[:, :], ALU.mult, ALU.max))
            end_phase()
            norm_stats(XTa, cur[:, 1:2], cur[:, 2:3])
        feature_to_node(XTa, S, C, ACT.Identity, aff[:, 0:1], aff[:, 1:2])
        layer_norm()

        s = Serial()
        s(dve, lambda: dve.tensor_copy(Sb[:, :, 0:D], Xb))
        s(sp, lambda: sp.dma_start(gin_rows.rearrange("(b p) f -> p b f", p=P), Xb), 16)
        s.wait(sp)
        end_phase()
        gcur = sb("gin_cur", len(GVECS))
        gv = {v: gcur[:, i:i + 1] for i, v in enumerate(GVECS)}
        with nc.Fori(0, GIN) as l:
            s = Serial()
            for i, name in enumerate(("L3_gnn_W1", "L3_gnn_W2")):
                s(sp, lambda: sp.dma_start(wst(6 + i), a[name][bass.ds(l, 1), :, :]
                                           .rearrange("a i o -> (a i) o")), 16)
            s(dve, lambda: dve.tensor_copy(gcur[:, :], vec[:, bass.ds(l * len(GVECS) + VB["Gb10"], len(GVECS))]))
            end_phase()
            gin_edges()
            node_to_feature(S, C, XTa)
            linear(XTa, wst(6), XTb, gv["b1"])
            norm_stats(XTb, gv["bn1_g"], gv["bn1_b"])
            linear(XTb, wst(7), XTa, gv["b2"], ACT.Relu, aff[:, 0:1], aff[:, 1:2])
            norm_stats(XTa, gv["bn2_g"], gv["bn2_b"])
            norm_stats(XTa, gv["bn3_g"], gv["bn3_b"], relu=True)
            feature_to_node(XTa, S, C, ACT.Relu, aff[:, 0:1], aff[:, 1:2], gin_rows)
        layer_norm()
        sp.dma_start(out[0:full * P, :].rearrange("(b p) f -> p b f", p=P), Xb[:, 0:full, :]).then_inc(q["out"], 16)
        sp.dma_start(out[full * P:N, :], Xb[0:N - full * P, full, :]).then_inc(q["out"], 16)
        sp.wait_ge(q["out"], 32)


INS = ["x", "src", "dst", "edge_attr_128", "edge_attr_3", "L0_gnn_W", "L0_gnn_attn_l", "L0_gnn_attn_r",
       "L1_gnn_global_feat", "L1_gnn_W_c", "L1_gnn_b_c", "L1_gnn_W1", "L1_gnn_b1", "L1_gnn_W2", "L1_gnn_b2",
       "L1_gnn_W3", "L1_gnn_b3"] + \
      [f"L2_gnn_{v}{l}" for l in (1, 2, 3) for v in ("W", "as", "ad", "We", "ae", "b", "g", "be")] + \
      ["L3_gnn_W1", "L3_gnn_W2"] + ["L3_gnn_" + v for v in GVECS]


def kernel(**inputs):
    import numpy as np
    import concourse.bacc as bacc
    from concourse.bass_utils import run_bass_kernel_spmd

    nc = bacc.Bacc("TRN2", target_bir_lowering=False, num_devices=1)
    arrays, aps = {}, {}
    for name in INS:
        v = np.ascontiguousarray(inputs[name])
        arrays["in_" + name] = v
        aps[name] = nc.dram_tensor("in_" + name, v.shape, mybir.dt.from_np(v.dtype), kind="ExternalInput").ap()
    out = nc.dram_tensor("out_0", (N, D), F32, kind="ExternalOutput").ap()
    build(nc, aps, out)
    r = run_bass_kernel_spmd(nc, [arrays], core_ids=[0])
    return r.results[0]["out_0"]
```
